# Optimizing a Trainium2 kernel written in Bass

```python
import numpy as np
import jax
import jax.numpy as jnp

def _softmax(x, axis=-1):
    return jax.nn.softmax(x, axis=axis)

def _gelu(x):
    return jax.nn.gelu(x, approximate=True)

def _silu(x):
    return jax.nn.silu(x)

def _sigmoid(x):
    return jax.nn.sigmoid(x)

def _layernorm(x, axis=-1, eps=1e-05):
    m = jnp.mean(x, axis=axis, keepdims=True)
    v = jnp.var(x, axis=axis, keepdims=True)
    return (x - m) / jnp.sqrt(v + eps)

def _scatter_add(tgt, idx, src, axis=0):
    return tgt.at[idx].add(src)

def _segment_sum(src, seg, n):
    return jax.ops.segment_sum(src, seg, n)
kernel_name = 'mk_xattn_ffn_d1_seqx_r8_e2489a'

def setup_inputs(seed: int=0):
    np.random.seed(seed)
    _w = jnp.asarray

    def _rec_inputs():
        import jax
        import jax.numpy as jnp
        _rk = jax.random.key(seed)
        x = 0.0002279 + 0.9999 * jax.random.normal(jax.random.fold_in(_rk, 1), (2, 512, 128), jnp.float32)
        _lenS = 512 - jax.random.randint(jax.random.fold_in(_rk, 7), (2,), 0, max(1, 512 // 4) + 1, jnp.int32)
        _lenS2 = 154 - jax.random.randint(jax.random.fold_in(_rk, 8), (2,), 0, max(1, 154 // 4) + 1, jnp.int32)
        _ctx_1024P = jax.random.normal(jax.random.fold_in(_rk, 11), (2, 16, 128), jnp.float32)
        _ctx_1024c = jax.random.dirichlet(jax.random.fold_in(_rk, 511), 0.3 * jnp.ones((16,), jnp.float32), (2, 154))
        _ctx_1024t = jnp.einsum('bsk,bkd->bsd', _ctx_1024c, _ctx_1024P)
        _ctx_1024t = _ctx_1024t * jax.lax.rsqrt(jnp.mean(jnp.square(_ctx_1024t)) + 1e-12) * 0.953939
        ctx_1024 = -7.10856e-05 + 0.999911 * (_ctx_1024t + 0.3 * jax.random.normal(jax.random.fold_in(_rk, 611), (2, 154, 128), jnp.float32))
        _validS = jnp.arange(512)[None, :] < _lenS[:, None]
        _validS2 = jnp.arange(154)[None, :] < _lenS2[:, None]
        _causal = jnp.tril(jnp.ones((512, 512), dtype=bool))
        mask_BxS2_bf1 = jnp.ones((2, 154), dtype=bool)
        return (x, ctx_1024, mask_BxS2_bf1)
    x, ctx_1024, mask_BxS2_bf1 = _rec_inputs()

    def _L0_xattn_setup():
        import jax, jax.numpy as jnp
        import numpy as np
        DIM = 128
        HEADS = 16
        DIM_HEAD = 64
        INNER = HEADS * DIM_HEAD
        B, F, Q = (16, 512, 64)
        EPS = 1e-05
        SCALE = DIM_HEAD ** (-0.5)

        def _layernorm(x, gamma, beta):
            mu = jnp.mean(x, axis=-1, keepdims=True)
            var = jnp.var(x, axis=-1, keepdims=True)
            return (x - mu) * jax.lax.rsqrt(var + EPS) * gamma + beta
        key = jax.random.key(seed)
        ks = jax.random.split(key, 8)
        features = jax.random.normal(ks[0], (B, F, DIM), dtype=jnp.float32)
        masks = jnp.ones((B, F), dtype=bool)
        latents = jax.random.normal(ks[1], (B, Q, DIM), dtype=jnp.float32)
        Wq = jax.random.normal(ks[2], (DIM, INNER), dtype=jnp.float32) / np.sqrt(DIM)
        Wk = jax.random.normal(ks[3], (DIM, INNER), dtype=jnp.float32) / np.sqrt(DIM)
        Wv = jax.random.normal(ks[4], (DIM, INNER), dtype=jnp.float32) / np.sqrt(DIM)
        Wo = jax.random.normal(ks[5], (INNER, DIM), dtype=jnp.float32) / np.sqrt(INNER)
        gm = jnp.ones((DIM,), jnp.float32)
        bm = jnp.zeros((DIM,), jnp.float32)
        gl = jnp.ones((DIM,), jnp.float32)
        bl = jnp.zeros((DIM,), jnp.float32)
        return {'features': features, 'masks': masks, 'latents': latents, 'gm': gm, 'bm': bm, 'gl': gl, 'bl': bl, 'Wq': Wq, 'Wk': Wk, 'Wv': Wv, 'Wo': Wo}
    _L0_xattn_all = _L0_xattn_setup()
    _L0_xattn_in = {k: v for k, v in _L0_xattn_all.items() if k in ('gm', 'bm', 'gl', 'bl', 'Wq', 'Wk', 'Wv', 'Wo')}
    del _L0_xattn_all

    def _L0_ffn_setup():
        import jax, jax.numpy as jnp
        import numpy as np
        DIM = 128
        INTER = 64
        E = 16
        TOPK = 4
        N_GROUPS = 4
        TOPK_GROUPS = 2
        ROUTE_SCALE = 1.0
        INIT_STD = 0.02
        B, S = (2, 128)
        key = jax.random.key(seed)
        ks = jax.random.split(key, 8)
        return {'x': jax.random.normal(ks[0], (B, S, DIM), jnp.float32), 'gate_w': jax.random.normal(ks[1], (E, DIM), jnp.float32) * INIT_STD, 'gate_bias': jnp.zeros((E,), jnp.float32), 'w1': jax.random.normal(ks[2], (E, INTER, DIM), jnp.float32) * INIT_STD, 'w2': jax.random.normal(ks[3], (E, DIM, INTER), jnp.float32) * INIT_STD, 'w3': jax.random.normal(ks[4], (E, INTER, DIM), jnp.float32) * INIT_STD, 'ws1': jax.random.normal(ks[5], (INTER, DIM), jnp.float32) * INIT_STD, 'ws2': jax.random.normal(ks[6], (DIM, INTER), jnp.float32) * INIT_STD, 'ws3': jax.random.normal(ks[7], (INTER, DIM), jnp.float32) * INIT_STD}
    _L0_ffn_all = _L0_ffn_setup()
    _L0_ffn_in = {k: v for k, v in _L0_ffn_all.items() if k in ('gate_w', 'gate_bias', 'w1', 'w2', 'w3', 'ws1', 'ws2', 'ws3')}
    del _L0_ffn_all
    return {'x': x, 'ctx_1024': ctx_1024, 'mask_BxS2_bf1': mask_BxS2_bf1, 'L0_xattn_gm': _L0_xattn_in['gm'], 'L0_xattn_bm': _L0_xattn_in['bm'], 'L0_xattn_gl': _L0_xattn_in['gl'], 'L0_xattn_bl': _L0_xattn_in['bl'], 'L0_xattn_Wq': _L0_xattn_in['Wq'], 'L0_xattn_Wk': _L0_xattn_in['Wk'], 'L0_xattn_Wv': _L0_xattn_in['Wv'], 'L0_xattn_Wo': _L0_xattn_in['Wo'], 'L0_ffn_gate_w': _L0_ffn_in['gate_w'], 'L0_ffn_gate_bias': _L0_ffn_in['gate_bias'], 'L0_ffn_w1': _L0_ffn_in['w1'], 'L0_ffn_w2': _L0_ffn_in['w2'], 'L0_ffn_w3': _L0_ffn_in['w3'], 'L0_ffn_ws1': _L0_ffn_in['ws1'], 'L0_ffn_ws2': _L0_ffn_in['ws2'], 'L0_ffn_ws3': _L0_ffn_in['ws3']}

def reference(x, ctx_1024, mask_BxS2_bf1, L0_xattn_gm, L0_xattn_bm, L0_xattn_gl, L0_xattn_bl, L0_xattn_Wq, L0_xattn_Wk, L0_xattn_Wv, L0_xattn_Wo, L0_ffn_gate_w, L0_ffn_gate_bias, L0_ffn_w1, L0_ffn_w2, L0_ffn_w3, L0_ffn_ws1, L0_ffn_ws2, L0_ffn_ws3):
    import jax
    import jax.numpy as jnp

    def _L0_xattn_ref(features, masks, latents, gm, bm, gl, bl, Wq, Wk, Wv, Wo):
        import jax, jax.numpy as jnp
        import numpy as np
        DIM = 128
        HEADS = 16
        DIM_HEAD = 64
        INNER = HEADS * DIM_HEAD
        B, F, Q = (16, 512, 64)
        EPS = 1e-05
        SCALE = DIM_HEAD ** (-0.5)

        def _layernorm(x, gamma, beta):
            mu = jnp.mean(x, axis=-1, keepdims=True)
            var = jnp.var(x, axis=-1, keepdims=True)
            return (x - mu) * jax.lax.rsqrt(var + EPS) * gamma + beta
        b, f, d = features.shape
        q_len = latents.shape[1]
        x = _layernorm(features, gm, bm)
        lat = _layernorm(latents, gl, bl)
        q = (lat @ Wq).reshape(b, q_len, HEADS, DIM_HEAD).transpose(0, 2, 1, 3)
        kv_input = jnp.concatenate([x, lat], axis=1)
        kv_mask = jnp.concatenate([masks, jnp.ones((b, q_len), dtype=bool)], axis=1)
        kv_mask = kv_mask[:, None, None, :]
        k = (kv_input @ Wk).reshape(b, f + q_len, HEADS, DIM_HEAD).transpose(0, 2, 1, 3)
        v = (kv_input @ Wv).reshape(b, f + q_len, HEADS, DIM_HEAD).transpose(0, 2, 1, 3)
        q = q * SCALE
        sim = jnp.einsum('bhqd,bhfd->bhqf', q, k)
        sim = sim - jax.lax.stop_gradient(jnp.max(sim, axis=-1, keepdims=True))
        sim = jnp.where(kv_mask, sim, -jnp.inf)
        alphas = jax.nn.softmax(sim, axis=-1)
        out = jnp.einsum('bhqf,bhfd->bhqd', alphas, v)
        out = out.transpose(0, 2, 1, 3).reshape(b, q_len, INNER)
        return out @ Wo

    def _L0_ffn_ref(x, gate_w, gate_bias, w1, w2, w3, ws1, ws2, ws3):
        import jax, jax.numpy as jnp
        import numpy as np
        DIM = 128
        INTER = 64
        E = 16
        TOPK = 4
        N_GROUPS = 4
        TOPK_GROUPS = 2
        ROUTE_SCALE = 1.0
        INIT_STD = 0.02
        B, S = (2, 128)
        Bx, Sx, D = x.shape
        T = Bx * Sx
        xf = x.reshape(T, D)
        scores = jax.nn.sigmoid(xf @ gate_w.T)
        original_scores = scores
        s = scores + gate_bias
        sg = s.reshape(T, N_GROUPS, E // N_GROUPS)
        group_scores = sg.max(axis=-1)
        _, gidx = jax.lax.top_k(group_scores, TOPK_GROUPS)
        keep = jnp.zeros((T, N_GROUPS), bool).at[jnp.arange(T)[:, None], gidx].set(True)
        s_masked = jnp.where(keep[:, :, None], sg, -jnp.inf).reshape(T, E)
        _, idx = jax.lax.top_k(s_masked, TOPK)
        weights = jnp.take_along_axis(original_scores, idx, axis=1) * ROUTE_SCALE
        comb = jnp.zeros((T, E), x.dtype).at[jnp.arange(T)[:, None], idx].add(weights)
        h1 = jnp.einsum('td,eid->tei', xf, w1)
        h3 = jnp.einsum('td,eid->tei', xf, w3)
        h = jax.nn.silu(h1) * h3
        y = jnp.einsum('tei,edi,te->td', h, w2, comb)
        z = jax.nn.silu(xf @ ws1.T) * (xf @ ws3.T) @ ws2.T
        return (y + z).reshape(Bx, Sx, D)
    x = x + _L0_xattn_ref(ctx_1024, mask_BxS2_bf1, _layernorm(x, axis=-1), L0_xattn_gm, L0_xattn_bm, L0_xattn_gl, L0_xattn_bl, L0_xattn_Wq, L0_xattn_Wk, L0_xattn_Wv, L0_xattn_Wo)
    x = x + _L0_ffn_ref(_layernorm(x, axis=-1), L0_ffn_gate_w, L0_ffn_gate_bias, L0_ffn_w1, L0_ffn_w2, L0_ffn_w3, L0_ffn_ws1, L0_ffn_ws2, L0_ffn_ws3)
    return x

_drawn_inputs = setup_inputs


def setup_inputs(seed=0):
    import zlib

    import numpy as np

    out = dict(_drawn_inputs(seed))
    spreads = {'L0_xattn_gm': (1.0, 0.553),
     'L0_xattn_bm': (0.0, 0.37),
     'L0_xattn_gl': (1.0, 0.2),
     'L0_xattn_bl': (0.0, 0.1),
     'L0_ffn_gate_bias': (0.0, 0.8)}
    factors = {'L0_ffn_gate_w': 8.0,
     'L0_ffn_w1': 8.0,
     'L0_ffn_w2': 8.0,
     'L0_ffn_w3': 8.0,
     'L0_ffn_ws1': 8.0,
     'L0_ffn_ws2': 8.0,
     'L0_ffn_ws3': 8.0}
    for name, (base, spread) in spreads.items():
        noise = np.random.default_rng([zlib.crc32(name.encode()), seed]).standard_normal(out[name].shape)
        drawn = base * np.exp(spread * noise) if base else spread * noise
        out[name] = jnp.asarray(drawn.astype(out[name].dtype))
    for name, factor in factors.items():
        out[name] = (out[name] * factor).astype(out[name].dtype)
    return out
```

```python
from contextlib import ExitStack

import concourse.bass as bass
from concourse import mybir

F32 = mybir.dt.float32
F32R = mybir.dt.float32r
BF16 = mybir.dt.bfloat16
U8 = mybir.dt.uint8
ACT = mybir.ActivationFunctionType
ALU = mybir.AluOpType
AX = mybir.AxisListType

P = 128
B, S, D = 2, 512, 128
CTX = 154
HEADS, DH = 16, 64
PAIRS = HEADS // 2
UNITS = B * PAIRS
SCALE = DH ** -0.5
EPS = 1e-5
QT = S // P
REM = CTX - P
RW = 32
MAIN = P + S
KT = MAIN // P
KEYS = MAIN + RW
HALF = KEYS // 2
C_MAIN, C_LAT, C_REM2 = RW, RW + P, RW + MAIN
C_ALL = C_REM2 + 2 * RW
E_N, INTER = 16, 64
GROUPS, TOPK_GROUPS, TOPK = 4, 2, 4
GE = E_N // GROUPS
CH = E_N * INTER // P
W13 = (E_N + 1) * INTER
BIG = 1e30
STU = 1 + 2 * KT


def build(nc, ctx, xt, xT, cx, mask, lngb, wqkv, wo, gate_w, gate_b, w1, w3, w2, ws2, ident, sel, own, out):
    def sb(name, shape, dt=F32):
        return ctx.enter_context(nc.sbuf_tensor(name, shape, dt))

    def sem(name):
        return ctx.enter_context(nc.semaphore(name))

    x_tok = sb("x_tok", [P, B * QT, D])
    c_tok = sb("c_tok", [P, B, 2, D])
    acc = sb("acc", [P, B, S])
    gb = sb("gb", [P, 4])
    mrow_u8 = sb("mrow_u8", [P, B, CTX], U8)
    mcol_u8 = sb("mcol_u8", [P, B, 2], U8)
    valid = sb("valid", [P, B, P + RW])
    lat0 = sb("lat0", [P, B, P + RW])
    kbias = sb("kbias", [P, B, 2])
    idf = sb("idf", [P, P])
    idb = sb("idb", [P, P], BF16)
    ones = sb("ones", [P, DH])
    eps = sb("eps", [P, 1])
    stats = sb("stats", [P, B, 6, 6])
    mv = sb("mv", [P, B, 6, 2])
    sd = sb("sd", [P, B, 6])
    kvT = sb("kvT", [P, B, C_ALL])
    wq = sb("wq", [P, 3, P])
    wop = sb("wop", [P, D])
    own_f = sb("own_f", [DH + 4, 2, KEYS])
    QA = [sb(f"QA{u}", [P, 2, S], F32R) for u in range(2)]
    QB = [sb(f"QB{u}", [DH + 4, 2, S], F32R) for u in range(2)]
    KA = [sb(f"KA{u}", [P, 2, MAIN + P], F32R) for u in range(2)]
    KB = [sb(f"KB{u}", [DH + 4, 2, MAIN + P], F32R) for u in range(2)]
    V = [sb(f"V{u}", [P, KT, P]) for u in range(2)]
    VR = [sb(f"VR{u}", [P, P]) for u in range(2)]
    nm = sb("nm", [P, QT, 2])
    nmp = sb("nmp", [P, QT, 2, 2], BF16)
    PR = [sb(f"PR{u}", [P, KT, 2, S]) for u in range(2)]
    PRr = [sb(f"PRr{u}", [P, S]) for u in range(2)]
    SUM = [sb(f"SUM{u}", [P, 2, S]) for u in range(2)]
    oraw = sb("oraw", [P, S])
    rden = sb("rden", [P, S])
    on = sb("on", [P, S])
    gw = sb("gw", [P, E_N])
    gbias = sb("gbias", [P, E_N])
    w1s = sb("w1s", [P, W13])
    w3s = sb("w3s", [P, W13])
    w2s = sb("w2s", [P, CH + 1, D])
    sel_f = sb("sel_f", [80, CH * P])
    sel_b = sb("sel_b", [80, CH * P], BF16)
    low16 = sb("low16", [P, E_N, E_N])
    x2n = sb("x2n", [P, QT, D])
    x2T = sb("x2T", [P, B, S])
    sc = sb("sc", [P, QT, E_N])
    sm_ = sb("sm_", [P, QT, E_N])
    gmx = sb("gmx", [P, QT, GROUPS])
    cmp_g = sb("cmp_g", [P, QT, GROUPS, GROUPS])
    eq_g = sb("eq_g", [P, QT, GROUPS, GROUPS])
    keep = sb("keep", [P, QT, GROUPS])
    cmp_e = sb("cmp_e", [P, QT, E_N, E_N])
    eq_e = sb("eq_e", [P, QT, E_N, E_N])
    rank = sb("rank", [P, QT, E_N])
    comb = sb("comb", [P, QT, E_N])
    cparts = [sb(f"cparts{b}", [80, S], BF16) for b in range(B)]
    cres = sb("cres", [E_N, S])
    sil = [sb(f"sil{u}", [P, S]) for u in range(2)]
    hT = [sb(f"hT{u}", [P, S]) for u in range(2)]
    res = sb("res", [P, B, S])

    def pb(name, banks):
        return ctx.enter_context(nc.psum_tensor(name, [P, banks * 512], F32))

    psM = pb("psM", 2)
    psT = pb("psT", 2)
    psJ = pb("psJ", 2)
    psO = pb("psO", 1)
    psX = pb("psX", 1)
    psM2 = psM[:, :].rearrange("p (a n) -> p a n", a=2)

    ld_x, ld_c, ld_s, ld_k, ld_w, ld_f = (sem(n) for n in ("ld_x", "ld_c", "ld_s", "ld_k", "ld_w", "ld_f"))
    ld_qkv, ld_wo = sem("ld_qkv"), sem("ld_wo")
    pre_act, pre_dve, pre_pe, pre_pool = sem("pre_act"), sem("pre_dve"), sem("pre_pe"), sem("pre_pool")
    rows_normed, kv_ready, consts_ready = sem("rows_normed"), sem("kv_ready"), sem("consts_ready")
    k_done, q_done, v_done = sem("k_done"), sem("q_done"), sem("v_done")
    sm_done, mrow_done, st_done, pv_done = sem("sm_done"), sem("mrow_done"), sem("st_done"), sem("pv_done")
    den_done, wo_done = sem("den_done"), sem("wo_done")
    m_out, o_out, q_hi, k_hi, qk_copied, v_out, exp_done = (
        sem(n) for n in ("m_out", "o_out", "q_hi", "k_hi", "qk_copied", "v_out", "exp_done"))
    q_lo, k_lo, max_done, m_hi, m_split, rden_done, on_done, acc_done = (
        sem(n) for n in ("q_lo", "k_lo", "max_done", "m_hi", "m_split", "rden_done", "on_done", "acc_done"))
    sum_step, sum_done = sem("sum_step"), sem("sum_done")
    x2_turned, x2_back, gate_logits, comb_turned = (sem(n) for n in ("x2_turned", "x2_back", "gate_logits", "comb_turned"))
    x2_stats, x2_normed, comb_done, parts_done = (sem(n) for n in ("x2_stats", "x2_normed", "comb_done", "parts_done"))
    x2_sd, x2_ready, scores_done = sem("x2_sd"), sem("x2_ready"), sem("scores_done")
    up_done, cb_done, y_done = sem("up_done"), sem("cb_done"), sem("y_done")
    sil_done, h_part, h_done, res_done = sem("sil_done"), sem("h_part"), sem("h_done"), sem("res_done")
    stored = sem("stored")

    def turn_bank(b):
        return psJ[:, 0:512] if b == 0 else psX[:, :]

    def back_bank(b):
        return psJ[:, 512:1024] if b == 0 else psX[:, :]

    block = ctx.enter_context(nc.Block())

    LD_S = 3 + 4 * B
    PREP_POOL = 2 + 2 + 4 + 8 + 1

    @block.sync
    def _(sp):
        xv = xt.rearrange("(t p) d -> p t d", p=P)
        sp.dma_start(x_tok[:, 0:QT, :], xv[:, 0:QT, :]).then_inc(ld_x, 16)
        sp.dma_start(c_tok[:, :, 0, :], cx[:, 0:P, :].rearrange("b p d -> p b d")).then_inc(ld_c, 16)
        sp.dma_start(x_tok[:, QT:, :], xv[:, QT:, :]).then_inc(ld_x, 16)
        sp.dma_start(own_f[DH:DH + 4, :, :], own).then_inc(ld_k, 16)
        sp.dma_start(wq[:, :, :], wqkv[0]).then_inc(ld_qkv, 16)
        sp.dma_start(wop[:, :], wo[0]).then_inc(ld_wo, 16)
        sp.dma_start(acc[:, :, :], xT.rearrange("d (b s) -> d b s", b=B)).then_inc(ld_w, 16)
        sp.dma_start(gw[:, :], gate_w).then_inc(ld_f, 16)
        sp.dma_start(gbias[:, :], gate_b.partition_broadcast(P)).then_inc(ld_f, 16)
        sp.dma_start(w1s[:, :], w1).then_inc(ld_f, 16)
        sp.dma_start(w3s[:, :], w3).then_inc(ld_f, 16)
        sp.dma_start(w2s[:, 0:CH, :], w2.rearrange("(c p) d -> p c d", p=P)).then_inc(ld_f, 16)
        sp.dma_start(w2s[0:INTER, CH, :], ws2).then_inc(ld_f, 16)
        sp.dma_start(sel_f[:, :], sel).then_inc(ld_f, 16)
        with sp.Fori(1, PAIRS) as p:
            sp.wait_ge(v_done, 2 * p)
            sp.dma_start(wq[:, :, :], wqkv[bass.ds(p, 1)].rearrange("o k n m -> (o k) n m")).then_inc(ld_qkv, 16)
            sp.wait_ge(wo_done, 2 * p)
            sp.dma_start(wop[:, :], wo[bass.ds(p, 1)].rearrange("o k n -> (o k) n")).then_inc(ld_wo, 16)
        for b in range(B):
            sp.wait_ge(res_done, b + 1)
            sp.dma_start(out[:, b * S:(b + 1) * S], res[:, b, :]).then_inc(stored, 16)
        sp.wait_ge(stored, 16 * B)

    @block.gpsimd
    def _(pool):
        pool.dma_start(gb[:, :], lngb).then_inc(ld_s, 16)
        pool.dma_start(idf[:, :], ident).then_inc(ld_s, 16)
        nc.gpsimd.memset(c_tok[0:RW, :, 1, :], 0.0).then_inc(pre_pool, 1)
        nc.gpsimd.memset(mcol_u8[:, :, :], 0).then_inc(pre_pool, 1)
        pool.wait_ge(pre_pool, 2)
        pool.dma_start(c_tok[0:REM, :, 1, :], cx[:, P:CTX, :].rearrange("b p d -> p b d")).then_inc(ld_s, 16)
        for b in range(B):
            pool.dma_start(mrow_u8[:, b, :], mask[b].partition_broadcast(P)).then_inc(ld_s, 16)
            pool.dma_start(mcol_u8[:, b, 0:1], mask[b, 0:P].unsqueeze(1)).then_inc(ld_s, 16)
            for h in range(2):
                pool.dma_start(mcol_u8[RW * h:RW * h + REM, b, 1:2], mask[b, P:CTX].unsqueeze(1)).then_inc(ld_s, 16)
        nc.gpsimd.memset(eps[:, :], EPS).then_inc(pre_pool, 1)
        nc.gpsimd.memset(ones[:, :], 1.0).then_inc(pre_pool, 1)
        for u in range(2):
            nc.gpsimd.memset(VR[u][:, :], 0.0).then_inc(pre_pool, 1)
            nc.gpsimd.memset(cparts[u][:, :], 0.0).then_inc(pre_pool, 1)
        for u in range(2):
            for t, rows in ((KA[u], P), (KB[u], DH + 4)):
                nc.gpsimd.memset(t[0:rows, 0, KEYS:].bitcast(F32), 0.0).then_inc(pre_pool, 1)
                nc.gpsimd.memset(t[0:rows, 1, 0:RW].bitcast(F32), 0.0).then_inc(pre_pool, 1)
        nc.gpsimd.memset(low16[:, :, :], 1.0).then_inc(pre_pool, 1)
        pool.wait_ge(pre_pool, PREP_POOL)
        nc.gpsimd.affine_select(out=low16[:, :, :], in_=low16[:, :, :], compare_op=ALU.is_gt, fill=0.0, base=0,
                                pattern=[[1, E_N], [-1, E_N]], channel_multiplier=0).then_inc(pre_pool, 1)

        def sums(i, b):
            u = 2 * i + b
            step = u * 5
            s, pr, rest = SUM[b], PR[b], PRr[b]
            pool.wait_ge(exp_done, u * STU + 5)
            nc.gpsimd.tensor_tensor(s[:, :, :], pr[:, 0], pr[:, 1], ALU.add).then_inc(sum_step, 1)
            for h in range(2):
                pool.wait_ge(sum_step, step + 1 + h)
                r = slice(RW * h, RW * h + REM)
                nc.gpsimd.tensor_tensor(s[r, h, :], s[r, h, :], rest[r, :], ALU.add).then_inc(sum_step, 1)
            for t in range(2, KT):
                pool.wait_ge(exp_done, u * STU + 3 + 2 * t)
                pool.wait_ge(sum_step, step + 1 + t)
                nc.gpsimd.tensor_tensor(s[:, :, :], s[:, :, :], pr[:, t], ALU.add)\
                    .then_inc(sum_step if t < KT - 1 else sum_done, 1)

        for b in range(B):
            sums(0, b)
        with pool.Fori(1, PAIRS - 1) as i:
            for b in range(B):
                sums(i, b)
        for b in range(B):
            sums(PAIRS - 1, b)

    @block.scalar
    def _(act):
        act.wait_ge(pre_pool, 3)
        for b in range(B):
            act.wait_ge(pre_dve, 2 * b + 1)
            nc.scalar.activation(sd[:, b, :], mv[:, b, :, 1], ACT.Sqrt, bias=eps[:, 0:1]).then_inc(pre_act, 1)
            act.wait_ge(pre_dve, 2 * b + 2)
            nc.scalar.activation(sd[:, b, 0:QT], mv[:, b, 0:QT, 1], ACT.Sqrt, bias=eps[:, 0:1]).then_inc(pre_act, 1)

        def q_high(u, nb):
            act.wait_ge(q_done, u + 1)
            for h in range(2):
                nc.scalar.activation(QA[nb][0:DH, h, :], psM[DH * h:DH * h + DH, 0:S], ACT.Copy).then_inc(q_hi, 1)

        def k_high(u, nb, h):
            if h == 0:
                act.wait_ge(k_done, u + 1)
            dst = KA[nb][0:DH, h, RW * h:RW * h + KEYS]
            src = psJ[DH * h:DH * h + DH, (RW if h == 0 else 0):][:, 0:KEYS]
            nc.scalar.activation(dst, src, ACT.Copy).then_inc(k_hi, 1)

        def q_copy(u, nb, h):
            if h == 0:
                act.wait_ge(q_hi, 2 * u + 2)
            nc.scalar.activation(QB[nb][0:DH, h, :], QA[nb][0:DH, h, :].bitcast(F32), ACT.Copy)

        def k_copy(u, nb, h):
            if h == 0:
                act.wait_ge(k_hi, 2 * u + 2)
            dst = KA[nb][DH:P, h, RW * h:RW * h + KEYS]
            src = KA[nb][0:DH, h, RW * h:RW * h + KEYS]
            last = nc.scalar.activation(dst, src.bitcast(F32), ACT.Copy)
            if h == 1:
                last.then_inc(qk_copied, 1)

        def v_copy(u, nb):
            act.wait_ge(v_done, u + 1)
            nc.scalar.activation(V[nb][:, :, :].rearrange("p k n -> p (k n)"), psJ[:, 0:KT * P], ACT.Copy)
            for h in range(2):
                r = slice(RW * h, RW * h + REM)
                last = nc.scalar.activation(VR[nb][r, DH * h:DH * h + DH],
                                            psJ[r, KT * P + DH * h:KT * P + DH * h + DH], ACT.Copy)
            last.then_inc(v_out, 1)

        def exp_tile(u, b, n):
            act.wait_ge(st_done, u * STU + n + 1)
            bank = (b * STU + n) % 2
            src = psT[:, bank * 512:bank * 512 + S]
            if n == 0:
                last = nc.scalar.activation(PRr[b][:, :], src, ACT.Exp, bias=kbias[:, b, 1:2],
                                            scale=SCALE)
            elif n <= 2:
                last = nc.scalar.activation(PR[b][:, 0, n - 1, :], src, ACT.Exp, bias=kbias[:, b, 0:1], scale=SCALE)
            else:
                last = nc.scalar.activation(PR[b][:, (n - 1) // 2, (n - 1) % 2, :], src, ACT.Exp, scale=SCALE)
            last.then_inc(exp_done, 1)

        def o_copy(u):
            act.wait_ge(pv_done, u + 1)
            nc.scalar.activation(oraw[:, :], psO[:, :], ACT.Copy).then_inc(o_out, 1)

        def unit(i, b, prev=True, nxt=True):
            u = 2 * i + b
            act.wait_ge(mrow_done, u + 1)
            for h in range(2):
                last = nc.scalar.activation(QB[b][DH:DH + 4, h, :], psX[DH:DH + 4, :], ACT.Copy)
            last.then_inc(m_out, 1)
            if prev:
                o_copy(u - 1)
            if nxt:
                q_high(u + 1, 1 - b)
            exp_tile(u, b, 0)
            if nxt:
                k_high(u + 1, 1 - b, 0)
            exp_tile(u, b, 1)
            if nxt:
                k_high(u + 1, 1 - b, 1)
            exp_tile(u, b, 2)
            if nxt:
                q_copy(u + 1, 1 - b, 0)
                q_copy(u + 1, 1 - b, 1)
            exp_tile(u, b, 3)
            if nxt:
                k_copy(u + 1, 1 - b, 0)
            exp_tile(u, b, 4)
            if nxt:
                k_copy(u + 1, 1 - b, 1)
            exp_tile(u, b, 5)
            exp_tile(u, b, 6)
            if nxt:
                v_copy(u + 1, 1 - b)
            for n in range(7, STU):
                exp_tile(u, b, n)

        act.wait_ge(pre_pool, PREP_POOL)
        q_high(0, 0)
        k_high(0, 0, 0)
        k_high(0, 0, 1)
        q_copy(0, 0, 0)
        q_copy(0, 0, 1)
        k_copy(0, 0, 0)
        k_copy(0, 0, 1)
        v_copy(0, 0)
        act.wait_ge(consts_ready, 1)
        unit(0, 0, prev=False)
        unit(0, 1)
        with act.Fori(1, PAIRS - 1) as i:
            unit(i, 0)
            unit(i, 1)
        unit(PAIRS - 1, 0)
        unit(PAIRS - 1, 1, nxt=False)
        act.wait_ge(on_done, UNITS - 1)
        o_copy(UNITS - 1)

        for b in range(B):
            act.wait_ge(x2_stats, b + 1)
            nc.scalar.activation(sd[:, b, 0:QT], mv[:, b, 0:QT, 1], ACT.Sqrt, bias=eps[:, 0:1]).then_inc(x2_sd, 1)
            act.wait_ge(x2_back, b + 1)
            nc.scalar.activation(x2T[:, b, :], back_bank(b)[:, 0:S], ACT.Copy).then_inc(x2_ready, 1)
            act.wait_ge(gate_logits, b + 1)
            nc.scalar.activation(sc[:, :, :].rearrange("p t e -> p (t e)"), turn_bank(b)[:, 0:QT * E_N], ACT.Sigmoid)\
                .then_inc(scores_done, 1)
            for g in range(0, 3) if b == 0 else range(3, 2 * (CH + 1)):
                rows = P if g % (CH + 1) < CH else INTER
                act.wait_ge(up_done, g + 1)
                if g >= 2:
                    act.wait_ge(h_done, g - 1)
                nc.scalar.activation(sil[g % 2][0:rows, :], psM[0:rows, (g % 2) * 512:(g % 2) * 512 + S],
                                     ACT.Silu).then_inc(sil_done, 1)

    @block.vector
    def _(dve):
        link = [0]
        link_sem = sem("dve_link")

        def linked(ins):
            link[0] += 1
            ins.then_inc(link_sem, 1)
            dve.wait_ge(link_sem, link[0])

        dve.wait_ge(ld_x, 16)
        dve.wait_ge(ld_c, 16)
        dve.wait_ge(ld_s, 16 * LD_S)
        nc.vector.memset(mv[:, :, :, :], 1.0)
        linked(nc.vector.memset(stats[:, :, :, :], 0.0))

        def stats_of(b, tiles):
            for src, rows, k in tiles:
                last = nc.vector.bn_stats(stats[0:rows, b, k, :], src)
            linked(last)
            for src, rows, k in tiles:
                last = nc.vector.bn_aggr(mv[0:rows, b, k, :], stats[0:rows, b, k, :])
            return last

        def normed(b, tiles):
            linked(nc.vector.reciprocal(sd[:, b, 0:len(tiles)], sd[:, b, 0:len(tiles)]))
            for src, rows, k in tiles:
                last = nc.vector.tensor_scalar(src, src, mv[0:rows, b, k, 0:1], sd[0:rows, b, k:k + 1],
                                               ALU.subtract, ALU.mult)
            return last

        for b in range(B):
            lat = [(x_tok[:, QT * b + t, :], P, t) for t in range(QT)]
            con = [(c_tok[:, b, 0, :], P, QT), (c_tok[0:REM, b, 1, :], REM, QT + 1)]
            if b == 1:
                dve.wait_ge(ld_x, 32)
            stats_of(b, lat + con).then_inc(pre_dve, 1)
            dve.wait_ge(pre_act, 2 * b + 1)
            linked(normed(b, lat + con))
            stats_of(b, lat).then_inc(pre_dve, 1)
            dve.wait_ge(pre_act, 2 * b + 2)
            normed(b, lat).then_inc(rows_normed, 1)

        dve.wait_ge(ld_s, 16 * LD_S)
        nc.vector.tensor_scalar(kbias[:, :, :], mcol_u8[:, :, :], -1.0, BIG, ALU.add, ALU.mult).then_inc(consts_ready, 1)
        nc.vector.memset(valid[:, :, CTX:], 0.0)
        linked(nc.vector.tensor_copy(valid[:, :, 0:CTX], mrow_u8[:, :, :]))
        nc.vector.tensor_copy(idb[:, :], idf[:, :])
        dve.wait_ge(ld_k, 16)
        for u in range(2):
            for h in range(2):
                last = nc.vector.tensor_copy(KB[u][DH:DH + 4, h, RW * h:RW * h + KEYS], own_f[DH:DH + 4, h, :])
        last.then_inc(consts_ready, 1)

        for b in range(B):
            dve.wait_ge(pre_pe, 2 * b + 1)
            linked(nc.vector.tensor_scalar(kvT[:, b, C_LAT:C_LAT + S], psM[:, 512 * b:512 * b + S],
                                           gb[:, 2:3], gb[:, 3:4], ALU.mult, ALU.add))
            dve.wait_ge(pre_pe, 2 * b + 2)
            cT = kvT[:, b, C_LAT - P - RW:C_LAT]
            src = psT[:, 512 * b:512 * b + P + RW]
            nc.vector.tensor_scalar(lat0[:, b, :], valid[:, b, :], -1.0, 1.0, ALU.mult, ALU.add)
            linked(nc.vector.tensor_scalar(cT, src, gb[:, 0:1], gb[:, 1:2], ALU.mult, ALU.add))
            linked(nc.vector.tensor_scalar(lat0[:, b, :], lat0[:, b, :], kvT[:, b, C_LAT:C_LAT + 1], None, ALU.mult))
            linked(nc.vector.tensor_tensor(cT[:, RW:], cT[:, RW:], valid[:, b, 0:P], ALU.mult))
            linked(nc.vector.tensor_tensor(cT[:, 0:RW], cT[:, 0:RW], valid[:, b, P:], ALU.mult))
            linked(nc.vector.tensor_tensor(cT[:, RW:], cT[:, RW:], lat0[:, b, 0:P], ALU.add))
            linked(nc.vector.tensor_tensor(cT[:, 0:RW], cT[:, 0:RW], lat0[:, b, P:], ALU.add))
            nc.vector.tensor_copy(kvT[:, b, C_REM2:C_REM2 + RW], cT[:, 0:RW])
            nc.vector.tensor_copy(kvT[:, b, C_REM2 + RW:], cT[:, 0:RW]).then_inc(kv_ready, 1)

        def qk_low(u, nb):
            for h in range(2):
                dve.wait_ge(q_hi, 2 * u + h + 1)
                last = nc.vector.tensor_tensor(QA[nb][DH:P, h, :], psM[DH * h:DH * h + DH, 0:S],
                                               QA[nb][0:DH, h, :].bitcast(F32), ALU.subtract)
            last.then_inc(q_lo, 1)
            for h in range(2):
                dve.wait_ge(k_hi, 2 * u + h + 1)
                cols = slice(RW * h, RW * h + KEYS)
                src = psJ[DH * h:DH * h + DH, (RW if h == 0 else 0):][:, 0:KEYS]
                last = nc.vector.tensor_tensor(KB[nb][0:DH, h, cols], src, KA[nb][0:DH, h, cols].bitcast(F32),
                                               ALU.subtract)
            last.then_inc(k_lo, 1)

        def norm_out(u):
            dve.wait_ge(den_done, u + 1)
            nc.vector.reciprocal(rden[:, :], psX[:, :]).then_inc(rden_done, 1)
            dve.wait_ge(rden_done, u + 1)
            dve.wait_ge(o_out, u + 1)
            nc.vector.tensor_tensor(on[:, :], oraw[:, :], rden[:, :], ALU.mult).then_inc(on_done, 1)

        def maxima(u, ns):
            for n in ns:
                dve.wait_ge(sm_done, u * 2 * QT + n + 1)
                nc.vector.tensor_reduce(nm[:, n % QT, n // QT:n // QT + 1], psM2[:, :, 0:HALF], AX.XY, ALU.max,
                                        negate=True).then_inc(max_done, 1)

        def split_max(u):
            dve.wait_ge(max_done, (u + 1) * 2 * QT)
            nc.vector.tensor_copy(nmp[:, :, :, 0], nm[:, :, :]).then_inc(m_hi, 1)
            dve.wait_ge(m_hi, u + 1)
            nc.vector.tensor_tensor(nmp[:, :, :, 1], nm[:, :, :], nmp[:, :, :, 0], ALU.subtract).then_inc(m_split, 1)

        def add_out(u, b):
            dve.wait_ge(wo_done, u + 1)
            nc.vector.tensor_tensor(acc[:, b, :], acc[:, b, :], psX[:, :], ALU.add).then_inc(acc_done, 1)

        def unit(i, b, prev=True, nxt=True):
            u = 2 * i + b
            if nxt:
                qk_low(u + 1, 1 - b)
            if prev:
                norm_out(u - 1)
            if nxt:
                maxima(u + 1, range(0, 7))
            if prev:
                add_out(u - 1, 1 - b)
            if nxt:
                maxima(u + 1, range(7, 2 * QT))
                split_max(u + 1)

        qk_low(0, 0)
        maxima(0, range(2 * QT))
        split_max(0)
        dve.wait_ge(ld_w, 16)
        unit(0, 0, prev=False)
        unit(0, 1)
        with dve.Fori(1, PAIRS - 1) as i:
            unit(i, 0)
            unit(i, 1)
        unit(PAIRS - 1, 0)
        unit(PAIRS - 1, 1, nxt=False)

        def low(n):
            return low16[:, 0:n, 0:n]

        def gate_groups(b):
            dve.wait_ge(scores_done, b + 1)
            linked(nc.vector.tensor_tensor(sm_[:, :, :], sc[:, :, :], gbias[:, :].unsqueeze(1).broadcast_to([P, QT, E_N]),
                                           ALU.add))
            sg = sm_[:, :, :].rearrange("p t (g e) -> p t g e", g=GROUPS)
            linked(nc.vector.tensor_reduce(gmx[:, :, :], sg, AX.X, ALU.max))
            compare(gmx, cmp_g, eq_g, GROUPS)
            choose(cmp_g, eq_g, keep, GROUPS, TOPK_GROUPS)
            kb = keep[:, :, :].unsqueeze(3).broadcast_to([P, QT, GROUPS, GE])
            linked(nc.vector.tensor_tensor(sg, sg, kb, ALU.mult))
            linked(nc.vector.tensor_scalar(keep[:, :, :], keep[:, :, :], -1.0, BIG, ALU.add, ALU.mult))
            linked(nc.vector.tensor_tensor(sg, sg, kb, ALU.add))

        def gate_compare():
            compare(sm_, cmp_e, eq_e, E_N)

        def gate_choose():
            choose(cmp_e, eq_e, rank, E_N, TOPK)
            nc.vector.tensor_tensor(comb[:, :, :], sc[:, :, :], rank[:, :, :], ALU.mult).then_inc(comb_done, 1)

        def compare(vals, cmp, eq, n):
            for t in range(QT):
                other = vals[:, t, :].unsqueeze(1).broadcast_to([P, n, n])
                mine = vals[:, t, :].unsqueeze(2).broadcast_to([P, n, n])
                nc.vector.tensor_tensor(cmp[:, t], other, mine, ALU.is_gt)
                last = nc.vector.tensor_tensor(eq[:, t], other, mine, ALU.is_equal)
            linked(last)

        def choose(cmp, eq, dst, n, k):
            linked(nc.vector.tensor_tensor(eq[:, :, :, :], eq[:, :, :, :], low(n).unsqueeze(1).broadcast_to([P, QT, n, n]),
                                           ALU.mult))
            linked(nc.vector.tensor_tensor(cmp[:, :, :, :], cmp[:, :, :, :], eq[:, :, :, :], ALU.add))
            linked(nc.vector.tensor_reduce(dst[:, :, :], cmp[:, :, :, :], AX.X, ALU.add))
            linked(nc.vector.tensor_scalar(dst[:, :, :], dst[:, :, :], float(k), None, ALU.is_lt))

        def norm_tokens(b):
            dve.wait_ge(x2_turned, b + 1)
            src = turn_bank(b)
            tiles = [(src[:, P * t:P * t + P], P, t) for t in range(QT)]
            stats_of(b, tiles).then_inc(x2_stats, 1)
            dve.wait_ge(x2_sd, b + 1)
            linked(nc.vector.reciprocal(sd[:, b, 0:QT], sd[:, b, 0:QT]))
            for s_, rows, k in tiles:
                last = nc.vector.tensor_scalar(x2n[:, k, :], s_, mv[:, b, k, 0:1], sd[:, b, k:k + 1],
                                               ALU.subtract, ALU.mult)
            last.then_inc(x2_normed, 1)

        def spread_parts(b):
            dve.wait_ge(comb_turned, b + 1)
            src = back_bank(b)[0:E_N, 0:S]
            linked(nc.vector.tensor_copy(cparts[b][0:E_N, :], src))
            linked(nc.vector.tensor_tensor(cres[:, :], src, cparts[b][0:E_N, :], ALU.subtract))
            linked(nc.vector.tensor_copy(cparts[b][32:32 + E_N, :], cres[:, :]))
            nc.vector.tensor_tensor(cparts[b][64:64 + E_N, :], cres[:, :], cparts[b][32:32 + E_N, :], ALU.subtract)\
                .then_inc(parts_done, 1)

        def hidden(g):
            b, c = divmod(g, CH + 1)
            rows = P if c < CH else INTER
            dve.wait_ge(sil_done, g + 1)
            if g >= 2:
                dve.wait_ge(y_done, g - 1)
            h3 = psT[0:rows, (g % 2) * 512:(g % 2) * 512 + S]
            h = hT[g % 2][0:rows, :]
            if c == CH:
                nc.vector.tensor_tensor(h, sil[g % 2][0:rows, :], h3, ALU.mult).then_inc(h_done, 1)
                return
            nc.vector.tensor_tensor(h, sil[g % 2][0:rows, :], h3, ALU.mult).then_inc(h_part, 1)
            dve.wait_ge(h_part, g - b + 1)
            dve.wait_ge(cb_done, g - b + 1)
            nc.vector.tensor_tensor(h, h, psJ[:, (g % 2) * 512:(g % 2) * 512 + S], ALU.mult).then_inc(h_done, 1)

        def result(b):
            dve.wait_ge(y_done, (b + 1) * (CH + 1))
            nc.vector.tensor_tensor(res[:, b, :], acc[:, b, :], psO[:, :], ALU.add).then_inc(res_done, 1)

        dve.wait_ge(ld_f, 16 * 7)
        linked(nc.vector.tensor_copy(sel_b[:, :], sel_f[:, :]))
        norm_tokens(0)
        norm_out(UNITS - 1)
        add_out(UNITS - 1, 1)
        dve.wait_ge(pre_pool, PREP_POOL + 1)
        gate_groups(0)
        gate_compare()
        gate_choose()
        spread_parts(0)
        hidden(0)
        hidden(1)
        norm_tokens(1)
        hidden(2)
        hidden(3)
        gate_groups(1)
        hidden(4)
        gate_compare()
        hidden(5)
        gate_choose()
        hidden(6)
        spread_parts(1)
        for g in range(7, 2 * (CH + 1)):
            hidden(g)
            if g == CH:
                result(0)
        result(1)

    @block.tensor
    def _(pe):
        pe.wait_ge(ld_s, 16 * LD_S)
        for b in range(B):
            pe.wait_ge(rows_normed, b + 1)
            for t in range(QT):
                last = nc.tensor.transpose(psM[:, 512 * b + P * t:512 * b + P * t + P], x_tok[:, QT * b + t, :], idf[:, :])
            last.then_inc(pre_pe, 1)
            nc.tensor.transpose(psT[:, 512 * b:512 * b + RW], c_tok[0:RW, b, 1, :], idf[0:RW, 0:RW])
            nc.tensor.transpose(psT[:, 512 * b + RW:512 * b + RW + P], c_tok[:, b, 0, :], idf[:, :]).then_inc(pre_pe, 1)

        def project_k(b):
            for lo, hi in ((0, 512), (512, C_MAIN + MAIN + RW)):
                last = nc.tensor.matmul(psJ[:, lo:hi], wq[:, 1, :], kvT[:, b, lo:hi], start=True, stop=True)
            last.then_inc(k_done, 1)

        def project_q(b):
            nc.tensor.matmul(psM[:, 0:S], wq[:, 0, :], kvT[:, b, C_LAT:C_LAT + S], start=True, stop=True)\
                .then_inc(q_done, 1)

        def project_v(u, b):
            pe.wait_ge(k_lo, u + 1)
            for t in range(KT):
                nc.tensor.matmul(psJ[:, P * t:P * t + P], kvT[:, b, C_MAIN + P * t:C_MAIN + P * t + P], wq[:, 2, :],
                                 start=True, stop=True)
            nc.tensor.matmul(psJ[0:2 * RW, MAIN:MAIN + P], kvT[:, b, C_REM2:C_REM2 + 2 * RW], wq[:, 2, :],
                             start=True, stop=True).then_inc(v_done, 1)

        def max_scores(u, b, n):
            h, t = divmod(n, QT)
            if n == 0:
                pe.wait_ge(q_lo, u + 1)
                pe.wait_ge(k_lo, u + 1)
                pe.wait_ge(qk_copied, u + 1)
            else:
                pe.wait_ge(max_done, u * 2 * QT + n)
            for a in range(2):
                lo = RW * h + HALF * a
                last = nc.tensor.matmul(psM[:, 512 * a:512 * a + HALF], QA[b][:, h, P * t:P * t + P],
                                        KA[b][:, h, lo:lo + HALF], start=True, stop=True)
            last.then_inc(sm_done, 1)

        def max_rows(u, b):
            pe.wait_ge(m_split, u + 1)
            for t in range(QT):
                last = nc.tensor.matmul(psX[DH:DH + 4, P * t:P * t + P], nmp[:, t, :, :].rearrange("p h a -> p (h a)"),
                                        idb[:, :], start=True, stop=True)
            last.then_inc(mrow_done, 1)

        def score_tile(u, b, n):
            bank = (b * STU + n) % 2
            dst = psT[:, bank * 512:bank * 512 + S]
            if n == 0:
                pe.wait_ge(m_out, u + 1)
                parts = [(0, MAIN), (1, 0)]
            else:
                if n >= 2:
                    pe.wait_ge(exp_done, u * STU + n - 1)
                h = (n - 1) % 2
                parts = [(h, RW * 2 * h + (n - 1) // 2 * P)]
            for j, (h, lo) in enumerate(parts):
                nc.tensor.matmul(dst, KA[b][:, h, lo:lo + P], QA[b][:, h, :], start=j == 0, stop=False)
                last = nc.tensor.matmul(dst, KB[b][:, h, lo:lo + P], QB[b][:, h, :], start=False, stop=j == len(parts) - 1)
            last.then_inc(st_done, 1)

        def weigh_values(u, b, j, prev=True):
            if j == 0:
                if prev:
                    pe.wait_ge(o_out, u)
                pe.wait_ge(v_out, u + 1)
            for h in range(2):
                cols = slice(DH * h, DH * h + DH)
                pe.wait_ge(exp_done, u * STU + (1 if j == 0 else 2 * j + h))
                if j == 0:
                    v, p = VR[b][:, cols], PRr[b][:, :]
                else:
                    v, p = V[b][:, j - 1, cols], PR[b][:, j - 1, h, :]
                last = nc.tensor.matmul(psO[cols, :], v, p, start=j == 0, stop=j == KT)
            if j == KT:
                last.then_inc(pv_done, 1)

        def denominators(u, b):
            pe.wait_ge(sum_done, u + 1)
            for h in range(2):
                last = nc.tensor.matmul(psX[DH * h:DH * h + DH, :], ones[:, :], SUM[b][:, h, :], start=True, stop=True)
            last.then_inc(den_done, 1)

        def project_out(u):
            pe.wait_ge(on_done, u + 1)
            nc.tensor.matmul(psX[:, :], wop[:, :], on[:, :], start=True, stop=True).then_inc(wo_done, 1)

        def unit(i, b, prev=True, nxt=True, first_pair=False):
            u = 2 * i + b
            if nxt:
                if b == 1:
                    pe.wait_ge(ld_qkv, 16 * (i + 2))
                pe.wait_ge(v_out, u + 1)
                project_k(1 - b)
            if not first_pair:
                pe.wait_ge(acc_done, u - 1)
            max_rows(u, b)
            if nxt:
                project_q(1 - b)
            score_tile(u, b, 0)
            for t in range(KT):
                score_tile(u, b, 1 + 2 * t)
                if nxt and t >= 2:
                    max_scores(u + 1, 1 - b, 2 * t - 3)
                score_tile(u, b, 2 + 2 * t)
                weigh_values(u, b, t, prev)
                if prev and t == 0:
                    denominators(u - 1, 1 - b)
                if nxt and t == 1:
                    project_v(u + 1, 1 - b)
                    max_scores(u + 1, 1 - b, 0)
                if nxt and t >= 2:
                    max_scores(u + 1, 1 - b, 2 * t - 2)
            weigh_values(u, b, KT, prev)
            if prev:
                if b == 1:
                    pe.wait_ge(ld_wo, 16 * (i + 1))
                project_out(u - 1)
            if nxt:
                max_scores(u + 1, 1 - b, 7)

        pe.wait_ge(kv_ready, 1)
        pe.wait_ge(consts_ready, 2)
        pe.wait_ge(ld_qkv, 16)
        project_q(0)
        project_k(0)
        project_v(0, 0)
        for n in range(2 * QT):
            max_scores(0, 0, n)
        pe.wait_ge(kv_ready, 2)
        unit(0, 0, prev=False, first_pair=True)
        unit(0, 1, first_pair=True)
        with pe.Fori(1, PAIRS - 1) as i:
            unit(i, 0)
            unit(i, 1)
        unit(PAIRS - 1, 0)
        unit(PAIRS - 1, 1, nxt=False)

        def turn(b):
            for t in range(QT):
                last = nc.tensor.transpose(turn_bank(b)[:, P * t:P * t + P], acc[:, b, P * t:P * t + P], idf[:, :])
            last.then_inc(x2_turned, 1)

        def turn_back(b):
            pe.wait_ge(x2_normed, b + 1)
            for t in range(QT):
                last = nc.tensor.transpose(back_bank(b)[:, P * t:P * t + P], x2n[:, t, :], idf[:, :])
            last.then_inc(x2_back, 1)

        def gate(b):
            pe.wait_ge(x2_ready, b + 1)
            for t in range(QT):
                last = nc.tensor.matmul(turn_bank(b)[:, E_N * t:E_N * t + E_N], x2T[:, b, P * t:P * t + P], gw[:, :],
                                        start=True, stop=True)
            last.then_inc(gate_logits, 1)

        def turn_comb(b):
            pe.wait_ge(comb_done, b + 1)
            for t in range(QT):
                last = nc.tensor.transpose(back_bank(b)[0:E_N, P * t:P * t + P], comb[:, t, :], idf[:, :])
            last.then_inc(comb_turned, 1)

        def up(g):
            b, c = divmod(g, CH + 1)
            rows = P if c < CH else INTER
            if g >= 2:
                pe.wait_ge(h_done, g - 1)
            for w, bank in ((w1s, psM), (w3s, psT)):
                last = nc.tensor.matmul(bank[0:rows, (g % 2) * 512:(g % 2) * 512 + S], w[:, P * c:P * c + rows],
                                        x2T[:, b, :], start=True, stop=True)
            last.then_inc(up_done, 1)

        def spread(g):
            b, c = divmod(g, CH + 1)
            if c < CH:
                nc.tensor.matmul(psJ[:, (g % 2) * 512:(g % 2) * 512 + S], sel_b[:, P * c:P * c + P], cparts[b][:, :],
                                 start=True, stop=True).then_inc(cb_done, 1)

        def down(g):
            b, c = divmod(g, CH + 1)
            rows = P if c < CH else INTER
            if g == CH + 1:
                pe.wait_ge(res_done, 1)
            pe.wait_ge(h_done, g + 1)
            nc.tensor.matmul(psO[:, :], w2s[0:rows, c, :], hT[g % 2][0:rows, :], start=c == 0, stop=c == CH)\
                .then_inc(y_done, 1)

        pe.wait_ge(acc_done, UNITS - 1)
        turn(0)
        denominators(UNITS - 1, 1)
        turn_back(0)
        pe.wait_ge(ld_f, 16 * 7)
        gate(0)
        pe.wait_ge(o_out, UNITS)
        project_out(UNITS - 1)
        up(0)
        up(1)
        pe.wait_ge(acc_done, UNITS)
        turn(1)
        turn_comb(0)
        pe.wait_ge(parts_done, 1)
        spread(0)
        spread(1)
        down(0)
        for g in range(2, 2 * (CH + 1)):
            up(g)
            if g == CH + 1:
                pe.wait_ge(parts_done, 2)
            spread(g)
            down(g - 1)
            if g == 2:
                turn_back(1)
                gate(1)
            if g == 7:
                turn_comb(1)
        down(2 * (CH + 1) - 1)


def kernel(x, ctx_1024, mask_BxS2_bf1, L0_xattn_gm, L0_xattn_bm, L0_xattn_gl, L0_xattn_bl, L0_xattn_Wq, L0_xattn_Wk,
           L0_xattn_Wv, L0_xattn_Wo, L0_ffn_gate_w, L0_ffn_gate_bias, L0_ffn_w1, L0_ffn_w2, L0_ffn_w3, L0_ffn_ws1,
           L0_ffn_ws2, L0_ffn_ws3):
    import concourse.bacc as bacc
    import numpy as np
    from concourse.bass_utils import run_bass_kernel_spmd

    a = np.asarray
    xt = a(x).reshape(B * S, D)

    def by_pair(w):
        return a(w).reshape(D, PAIRS, P)

    own = np.zeros((4, 2, KEYS), np.float32)
    own[0:2, 0], own[2:4, 1] = 1.0, 1.0
    sel = np.zeros((80, CH * P), np.float32)
    for part in range(3):
        for e in range(E_N):
            sel[32 * part + e, e * INTER:(e + 1) * INTER] = 1.0
    arrays = {
        "xt": xt,
        "xT": xt.T,
        "cx": a(ctx_1024),
        "mask": a(mask_BxS2_bf1).view(np.uint8),
        "lngb": np.stack([a(L0_xattn_gm), a(L0_xattn_bm), a(L0_xattn_gl), a(L0_xattn_bl)], axis=1),
        "wqkv": np.stack([by_pair(L0_xattn_Wq), by_pair(L0_xattn_Wk), by_pair(L0_xattn_Wv)], axis=2).transpose(1, 0, 2, 3),
        "wo": a(L0_xattn_Wo).reshape(PAIRS, P, D),
        "gate_w": a(L0_ffn_gate_w).T,
        "gate_b": a(L0_ffn_gate_bias),
        "w1": np.concatenate([a(L0_ffn_w1).transpose(2, 0, 1).reshape(D, E_N * INTER), a(L0_ffn_ws1).T], axis=1),
        "w3": np.concatenate([a(L0_ffn_w3).transpose(2, 0, 1).reshape(D, E_N * INTER), a(L0_ffn_ws3).T], axis=1),
        "w2": a(L0_ffn_w2).transpose(0, 2, 1).reshape(E_N * INTER, D),
        "ws2": a(L0_ffn_ws2).T,
        "ident": np.eye(P, dtype=np.float32),
        "sel": sel,
        "own": own,
    }
    arrays = {"in_" + k: np.ascontiguousarray(v) for k, v in arrays.items()}
    nc = bacc.Bacc("TRN2", target_bir_lowering=False, num_devices=1)
    aps = [nc.dram_tensor(k, v.shape, mybir.dt.from_np(v.dtype), kind="ExternalInput").ap() for k, v in arrays.items()]
    out = nc.dram_tensor("out_T", (D, B * S), F32, kind="ExternalOutput").ap()
    with ExitStack() as ctx:
        build(nc, ctx, *aps, out)
    got = run_bass_kernel_spmd(nc, [arrays], core_ids=[0]).results[0]["out_T"]
    return np.ascontiguousarray(got.T).reshape(B, S, D)
```

```python
from contextlib import ExitStack

import concourse.bass as bass
from concourse import mybir

F32 = mybir.dt.float32
F32R = mybir.dt.float32r
BF16 = mybir.dt.bfloat16
U8 = mybir.dt.uint8
ACT = mybir.ActivationFunctionType
ALU = mybir.AluOpType
AX = mybir.AxisListType

P = 128
B, S, D = 2, 512, 128
CTX = 154
HEADS, DH = 16, 64
PAIRS = HEADS // 2
UNITS = B * PAIRS
SCALE = DH ** -0.5
EPS = 1e-5
QT = S // P
REM = CTX - P
RW = 32
MAIN = P + S
KT = MAIN // P
KEYS = MAIN + RW
HALF = KEYS // 2
C_MAIN, C_LAT, C_REM2 = RW, RW + P, RW + MAIN
C_ALL = C_REM2 + 2 * RW
E_N, INTER = 16, 64
GROUPS, TOPK_GROUPS, TOPK = 4, 2, 4
GE = E_N // GROUPS
CH = E_N * INTER // P
W13 = (E_N + 1) * INTER
BIG = 1e30
STU = 1 + 2 * KT


def build(nc, ctx, xt, xT, cx, mask, lngb, wqkv, wo, gate_w, gate_b, w1, w3, w2, ws2, ident, sel, own, out):
    def sb(name, shape, dt=F32):
        return ctx.enter_context(nc.sbuf_tensor(name, shape, dt))

    def sem(name):
        return ctx.enter_context(nc.semaphore(name))

    x_tok = sb("x_tok", [P, B * QT, D])
    c_tok = sb("c_tok", [P, B, 2, D])
    acc = sb("acc", [P, B, S])
    gb = sb("gb", [P, 4])
    mrow_u8 = sb("mrow_u8", [P, B, CTX], U8)
    mcol_u8 = sb("mcol_u8", [P, B, 2], U8)
    valid = sb("valid", [P, B, P + RW])
    lat0 = sb("lat0", [P, B, P + RW])
    kbias = sb("kbias", [P, B, 2])
    idf = sb("idf", [P, P])
    idb = sb("idb", [P, P], BF16)
    ones = sb("ones", [P, DH])
    eps = sb("eps", [P, 1])
    stats = sb("stats", [P, B, 6, 6])
    mv = sb("mv", [P, B, 6, 2])
    sd = sb("sd", [P, B, 6])
    kvT = sb("kvT", [P, B, C_ALL])
    wq = sb("wq", [P, 3, P])
    wop = sb("wop", [P, D])
    own_f = sb("own_f", [DH + 4, 2, KEYS])
    QA = [sb(f"QA{u}", [P, 2, S], F32R) for u in range(2)]
    QB = [sb(f"QB{u}", [DH + 4, 2, S], F32R) for u in range(2)]
    KA = [sb(f"KA{u}", [P, 2, MAIN + P], F32R) for u in range(2)]
    KB = [sb(f"KB{u}", [DH + 4, 2, MAIN + P], F32R) for u in range(2)]
    V = [sb(f"V{u}", [P, KT, P]) for u in range(2)]
    VR = [sb(f"VR{u}", [P, P]) for u in range(2)]
    nm = sb("nm", [P, QT, 2])
    nmp = sb("nmp", [P, QT, 2, 2], BF16)
    PR = [sb(f"PR{u}", [P, KT, 2, S]) for u in range(2)]
    PRr = [sb(f"PRr{u}", [P, S]) for u in range(2)]
    SUM = [sb(f"SUM{u}", [P, 2, S]) for u in range(2)]
    oraw = sb("oraw", [P, S])
    rden = sb("rden", [P, S])
    on = sb("on", [P, S])
    gw = sb("gw", [P, E_N])
    gbias = sb("gbias", [P, E_N])
    w1s = sb("w1s", [P, W13])
    w3s = sb("w3s", [P, W13])
    w2s = sb("w2s", [P, CH + 1, D])
    sel_f = sb("sel_f", [80, CH * P])
    sel_b = sb("sel_b", [80, CH * P], BF16)
    low4 = sb("low4", [P, GROUPS, GROUPS])
    again = sb("again", [P, QT, E_N])
    top8 = sb("top8", [P, QT, 8])
    more = sb("more", [P, QT, E_N])
    same = sb("same", [P, QT, E_N])
    nth = sb("nth", [P, QT, E_N])
    left = sb("left", [P, QT, 1])
    x2n = sb("x2n", [P, QT, D])
    x2T = sb("x2T", [P, B, S])
    sc = sb("sc", [P, QT, E_N])
    sm_ = sb("sm_", [P, QT, E_N])
    gmx = sb("gmx", [P, QT, GROUPS])
    cmp_g = sb("cmp_g", [P, QT, GROUPS, GROUPS])
    eq_g = sb("eq_g", [P, QT, GROUPS, GROUPS])
    keep = sb("keep", [P, QT, GROUPS])
    comb = sb("comb", [P, QT, E_N])
    cparts = [sb(f"cparts{b}", [80, S], BF16) for b in range(B)]
    cres = sb("cres", [E_N, S])
    sil = [sb(f"sil{u}", [P, S]) for u in range(2)]
    hT = [sb(f"hT{u}", [P, S]) for u in range(2)]
    res = sb("res", [P, B, S])

    def pb(name, banks):
        return ctx.enter_context(nc.psum_tensor(name, [P, banks * 512], F32))

    psM = pb("psM", 2)
    psJ = pb("psJ", 2)
    psT = pb("psT", 2)
    psO = pb("psO", 1)
    psX = pb("psX", 1)
    psMJ = [t[:, :].rearrange("p (a n) -> p a n", a=2) for t in (psM, psJ)]

    ld_x, ld_c, ld_s, ld_k, ld_w, ld_f = (sem(n) for n in ("ld_x", "ld_c", "ld_s", "ld_k", "ld_w", "ld_f"))
    ld_qkv, ld_wo = sem("ld_qkv"), sem("ld_wo")
    var_ready, sd_ready, pre_pe, pre_pool = sem("var_ready"), sem("sd_ready"), sem("pre_pe"), sem("pre_pool")
    rows_normed, kv_ready, consts_ready = sem("rows_normed"), sem("kv_ready"), sem("consts_ready")
    k_done, q_done, v_done = sem("k_done"), sem("q_done"), sem("v_done")
    sm_done, mrow_done, st_done, pv_done = sem("sm_done"), sem("mrow_done"), sem("st_done"), sem("pv_done")
    den_done, wo_done = sem("den_done"), sem("wo_done")
    m_out, o_out, q_hi, k_hi, k_copied, v_out, exp_done = (
        sem(n) for n in ("m_out", "o_out", "q_hi", "k_hi", "k_copied", "v_out", "exp_done"))
    q_lo, k_lo, max_done, m_hi, m_split, rden_done, on_done, acc_done = (
        sem(n) for n in ("q_lo", "k_lo", "max_done", "m_hi", "m_split", "rden_done", "on_done", "acc_done"))
    sum_step, sum_done = sem("sum_step"), sem("sum_done")
    x2_turned, x2_back, gate_logits, comb_turned = (sem(n) for n in ("x2_turned", "x2_back", "gate_logits", "comb_turned"))
    x2_stats, x2_normed, comb_done, parts_done = (sem(n) for n in ("x2_stats", "x2_normed", "comb_done", "parts_done"))
    x2_sd, x2_ready, scores_done = sem("x2_sd"), sem("x2_ready"), sem("scores_done")
    up_done, cb_done, y_done = sem("up_done"), sem("cb_done"), sem("y_done")
    sil_done, h_part, h_done, res_done = sem("sil_done"), sem("h_part"), sem("h_done"), sem("res_done")
    stored = sem("stored")

    def turn_bank(b):
        return psM[:, 0:512] if b == 0 else psX[:, :]

    def back_bank(b):
        return psM[:, 512:1024] if b == 0 else psX[:, :]

    block = ctx.enter_context(nc.Block())

    LD_S = 2 + 4 * B
    PREP_POOL = 2 + 2 + 4 + 8 + 2
    PREP_MASK = PREP_POOL + 6

    @block.sync
    def _(sp):
        sp.dma_start(x_tok[:, :, :], xt.rearrange("(t p) d -> p t d", p=P)).then_inc(ld_x, 16)
        sp.dma_start(c_tok[:, :, 0, :], cx[:, 0:P, :].rearrange("b p d -> p b d")).then_inc(ld_c, 16)
        sp.wait_ge(pre_pool, 1)
        sp.dma_start(c_tok[0:REM, :, 1, :], cx[:, P:CTX, :].rearrange("b p d -> p b d")).then_inc(ld_c, 16)
        sp.dma_start(own_f[DH:DH + 4, :, :], own).then_inc(ld_k, 16)
        sp.dma_start(wq[:, :, :], wqkv[0]).then_inc(ld_qkv, 16)
        sp.dma_start(wop[:, :], wo[0]).then_inc(ld_wo, 16)
        sp.dma_start(acc[:, :, :], xT.rearrange("d (b s) -> d b s", b=B)).then_inc(ld_w, 16)
        sp.dma_start(gw[:, :], gate_w).then_inc(ld_f, 16)
        sp.dma_start(gbias[:, :], gate_b.partition_broadcast(P)).then_inc(ld_f, 16)
        sp.dma_start(w1s[:, :], w1).then_inc(ld_f, 16)
        sp.dma_start(w3s[:, :], w3).then_inc(ld_f, 16)
        sp.dma_start(w2s[:, 0:CH, :], w2.rearrange("(c p) d -> p c d", p=P)).then_inc(ld_f, 16)
        sp.dma_start(w2s[0:INTER, CH, :], ws2).then_inc(ld_f, 16)
        sp.dma_start(sel_f[:, :], sel).then_inc(ld_f, 16)
        sp.wait_ge(v_done, 2)
        sp.dma_start(wq[:, :, :], wqkv[1]).then_inc(ld_qkv, 16)
        with sp.Fori(1, PAIRS - 1) as p:
            sp.wait_ge(v_done, 2 * p + 2)
            sp.dma_start(wq[:, :, :], wqkv[bass.ds(p + 1, 1)].rearrange("o k n m -> (o k) n m")).then_inc(ld_qkv, 16)
            sp.wait_ge(wo_done, 2 * p)
            sp.dma_start(wop[:, :], wo[bass.ds(p, 1)].rearrange("o k n -> (o k) n")).then_inc(ld_wo, 16)
        sp.wait_ge(wo_done, 2 * (PAIRS - 1))
        sp.dma_start(wop[:, :], wo[PAIRS - 1]).then_inc(ld_wo, 16)
        for b in range(B):
            sp.wait_ge(res_done, b + 1)
            sp.dma_start(out[:, b * S:(b + 1) * S], res[:, b, :]).then_inc(stored, 16)
        sp.wait_ge(stored, 16 * B)

    @block.gpsimd
    def _(pool):
        nc.gpsimd.memset(c_tok[0:RW, :, 1, :], 0.0).then_inc(pre_pool, 1)
        nc.gpsimd.memset(mcol_u8[:, :, :], 0).then_inc(pre_pool, 1)
        pool.dma_start(idf[:, :], ident).then_inc(ld_s, 16)
        pool.dma_start(gb[:, :], lngb).then_inc(ld_s, 16)
        pool.wait_ge(pre_pool, 2)
        for b in range(B):
            pool.dma_start(mrow_u8[:, b, :], mask[b].partition_broadcast(P)).then_inc(ld_s, 16)
            pool.dma_start(mcol_u8[:, b, 0:1], mask[b, 0:P].unsqueeze(1)).then_inc(ld_s, 16)
            for h in range(2):
                pool.dma_start(mcol_u8[RW * h:RW * h + REM, b, 1:2], mask[b, P:CTX].unsqueeze(1)).then_inc(ld_s, 16)
        nc.gpsimd.memset(eps[:, :], EPS).then_inc(pre_pool, 1)
        nc.gpsimd.memset(ones[:, :], 1.0).then_inc(pre_pool, 1)
        for u in range(2):
            nc.gpsimd.memset(VR[u][:, :], 0.0).then_inc(pre_pool, 1)
            nc.gpsimd.memset(cparts[u][:, :], 0.0).then_inc(pre_pool, 1)
        for u in range(2):
            for t, rows in ((KA[u], P), (KB[u], DH + 4)):
                nc.gpsimd.memset(t[0:rows, 0, KEYS:].bitcast(F32), 0.0).then_inc(pre_pool, 1)
                nc.gpsimd.memset(t[0:rows, 1, 0:RW].bitcast(F32), 0.0).then_inc(pre_pool, 1)
        nc.gpsimd.memset(low4[:, :, :], 1.0).then_inc(pre_pool, 1)
        nc.gpsimd.memset(again[:, :, :], 1.0).then_inc(pre_pool, 1)
        pool.wait_ge(pre_pool, PREP_POOL)
        nc.gpsimd.memset(again[:, :, 0:1], 0.0).then_inc(pre_pool, 1)
        nc.gpsimd.affine_select(out=low4[:, :, :], in_=low4[:, :, :], compare_op=ALU.is_gt, fill=0.0, base=0,
                                pattern=[[1, GROUPS], [-1, GROUPS]], channel_multiplier=0).then_inc(pre_pool, 1)
        pool.wait_ge(ld_s, 16 * LD_S)
        nc.gpsimd.tensor_copy(valid[:, :, 0:CTX], mrow_u8[:, :, :]).then_inc(pre_pool, 1)
        nc.gpsimd.memset(valid[:, :, CTX:], 0.0).then_inc(pre_pool, 1)
        nc.gpsimd.tensor_scalar(kbias[:, :, :], mcol_u8[:, :, :], -1.0, BIG, ALU.add, ALU.mult).then_inc(pre_pool, 1)
        pool.wait_ge(pre_pool, PREP_POOL + 5)
        nc.gpsimd.tensor_scalar(lat0[:, :, :], valid[:, :, :], -1.0, 1.0, ALU.mult, ALU.add).then_inc(pre_pool, 1)

        def sums(i, b):
            u = 2 * i + b
            step = u * 5
            s, pr, rest = SUM[b], PR[b], PRr[b]
            pool.wait_ge(exp_done, u * STU + 5)
            nc.gpsimd.tensor_tensor(s[:, :, :], pr[:, 0], pr[:, 1], ALU.add).then_inc(sum_step, 1)
            for h in range(2):
                pool.wait_ge(sum_step, step + 1 + h)
                r = slice(RW * h, RW * h + REM)
                nc.gpsimd.tensor_tensor(s[r, h, :], s[r, h, :], rest[r, :], ALU.add).then_inc(sum_step, 1)
            for t in range(2, KT):
                pool.wait_ge(exp_done, u * STU + 3 + 2 * t)
                pool.wait_ge(sum_step, step + 1 + t)
                nc.gpsimd.tensor_tensor(s[:, :, :], s[:, :, :], pr[:, t], ALU.add)\
                    .then_inc(sum_step if t < KT - 1 else sum_done, 1)

        for b in range(B):
            sums(0, b)
        with pool.Fori(1, PAIRS - 1) as i:
            for b in range(B):
                sums(i, b)
        for b in range(B):
            sums(PAIRS - 1, b)

    @block.scalar
    def _(act):
        act.wait_ge(pre_pool, 3)
        for level in range(2):
            for b in range(B):
                act.wait_ge(var_ready, 2 * level + b + 1)
                n = QT if level else QT + 2
                nc.scalar.activation(sd[:, b, 0:n], mv[:, b, 0:n, 1], ACT.Sqrt, bias=eps[:, 0:1]).then_inc(sd_ready, 1)
        act.wait_ge(ld_s, 16 * LD_S)
        nc.scalar.activation(idb[:, :], idf[:, :], ACT.Copy)
        act.wait_ge(ld_k, 16)
        for u in range(2):
            for h in range(2):
                last = nc.scalar.activation(KB[u][DH:DH + 4, h, RW * h:RW * h + KEYS], own_f[DH:DH + 4, h, :], ACT.Copy)
        last.then_inc(consts_ready, 1)

        def q_high(u, nb):
            act.wait_ge(q_done, u + 1)
            for h in range(2):
                nc.scalar.activation(QA[nb][0:DH, h, :], psM[DH * h:DH * h + DH, 0:S], ACT.Copy).then_inc(q_hi, 1)

        def k_high(u, nb, h):
            if h == 0:
                act.wait_ge(k_done, u + 1)
            dst = KA[nb][0:DH, h, RW * h:RW * h + KEYS]
            src = psJ[DH * h:DH * h + DH, (RW if h == 0 else 0):][:, 0:KEYS]
            nc.scalar.activation(dst, src, ACT.Copy).then_inc(k_hi, 1)

        def q_copy(u, nb, h):
            if h == 0:
                act.wait_ge(q_hi, 2 * u + 2)
            nc.scalar.activation(QB[nb][0:DH, h, :], QA[nb][0:DH, h, :].bitcast(F32), ACT.Copy)

        def k_copy(u, nb, h):
            if h == 0:
                act.wait_ge(k_hi, 2 * u + 2)
            dst = KA[nb][DH:P, h, RW * h:RW * h + KEYS]
            src = KA[nb][0:DH, h, RW * h:RW * h + KEYS]
            last = nc.scalar.activation(dst, src.bitcast(F32), ACT.Copy)
            if h == 1:
                last.then_inc(k_copied, 1)

        def v_copy(u, nb):
            act.wait_ge(v_done, u + 1)
            nc.scalar.activation(V[nb][:, :, :].rearrange("p k n -> p (k n)"), psJ[:, 0:KT * P], ACT.Copy)
            for h in range(2):
                r = slice(RW * h, RW * h + REM)
                last = nc.scalar.activation(VR[nb][r, DH * h:DH * h + DH],
                                            psJ[r, KT * P + DH * h:KT * P + DH * h + DH], ACT.Copy)
            last.then_inc(v_out, 1)

        def exp_tile(u, b, n):
            act.wait_ge(st_done, u * STU + n + 1)
            bank = (b * STU + n) % 2
            src = psT[:, bank * 512:bank * 512 + S]
            if n == 0:
                last = nc.scalar.activation(PRr[b][:, :], src, ACT.Exp, bias=kbias[:, b, 1:2],
                                            scale=SCALE)
            elif n <= 2:
                last = nc.scalar.activation(PR[b][:, 0, n - 1, :], src, ACT.Exp, bias=kbias[:, b, 0:1], scale=SCALE)
            else:
                last = nc.scalar.activation(PR[b][:, (n - 1) // 2, (n - 1) % 2, :], src, ACT.Exp, scale=SCALE)
            last.then_inc(exp_done, 1)

        def o_copy(u):
            act.wait_ge(pv_done, u + 1)
            nc.scalar.activation(oraw[:, :], psO[:, :], ACT.Copy).then_inc(o_out, 1)

        def unit(i, b, prev=True, nxt=True, first_pair=False):
            u = 2 * i + b
            if prev:
                if not first_pair:
                    act.wait_ge(on_done, u - 1)
                o_copy(u - 1)
            act.wait_ge(mrow_done, u + 1)
            for h in range(2):
                last = nc.scalar.activation(QB[b][DH:DH + 4, h, :], psX[DH:DH + 4, :], ACT.Copy)
            last.then_inc(m_out, 1)
            if nxt:
                q_high(u + 1, 1 - b)
            exp_tile(u, b, 0)
            if nxt:
                k_high(u + 1, 1 - b, 0)
            exp_tile(u, b, 1)
            if nxt:
                k_high(u + 1, 1 - b, 1)
            exp_tile(u, b, 2)
            if nxt:
                k_copy(u + 1, 1 - b, 0)
            exp_tile(u, b, 3)
            if nxt:
                k_copy(u + 1, 1 - b, 1)
            exp_tile(u, b, 4)
            if nxt:
                v_copy(u + 1, 1 - b)
            exp_tile(u, b, 5)
            exp_tile(u, b, 6)
            if nxt:
                q_copy(u + 1, 1 - b, 0)
            exp_tile(u, b, 7)
            if nxt:
                q_copy(u + 1, 1 - b, 1)
            for n in range(8, STU):
                exp_tile(u, b, n)

        act.wait_ge(pre_pool, PREP_POOL)
        q_high(0, 0)
        k_high(0, 0, 0)
        k_high(0, 0, 1)
        k_copy(0, 0, 0)
        k_copy(0, 0, 1)
        v_copy(0, 0)
        q_copy(0, 0, 0)
        q_copy(0, 0, 1)
        act.wait_ge(pre_pool, PREP_MASK)
        unit(0, 0, prev=False, first_pair=True)
        unit(0, 1, first_pair=True)
        with act.Fori(1, PAIRS - 1) as i:
            unit(i, 0)
            unit(i, 1)
        unit(PAIRS - 1, 0)
        unit(PAIRS - 1, 1, nxt=False)
        act.wait_ge(on_done, UNITS - 1)
        o_copy(UNITS - 1)

        for b in range(B):
            act.wait_ge(x2_stats, b + 1)
            nc.scalar.activation(sd[:, b, 0:QT], mv[:, b, 0:QT, 1], ACT.Sqrt, bias=eps[:, 0:1]).then_inc(x2_sd, 1)
            act.wait_ge(x2_back, b + 1)
            nc.scalar.activation(x2T[:, b, :], back_bank(b)[:, 0:S], ACT.Copy).then_inc(x2_ready, 1)
            act.wait_ge(gate_logits, b + 1)
            nc.scalar.activation(sc[:, :, :].rearrange("p t e -> p (t e)"), turn_bank(b)[:, 0:QT * E_N], ACT.Sigmoid)\
                .then_inc(scores_done, 1)
            for g in range(0, 3) if b == 0 else range(3, 2 * (CH + 1)):
                rows = P if g % (CH + 1) < CH else INTER
                act.wait_ge(up_done, g + 1)
                if g >= 2:
                    act.wait_ge(h_done, g - 1)
                nc.scalar.activation(sil[g % 2][0:rows, :], psM[0:rows, (g % 2) * 512:(g % 2) * 512 + S],
                                     ACT.Silu).then_inc(sil_done, 1)

    @block.vector
    def _(dve):
        link = [0]
        link_sem = sem("dve_link")

        def linked(ins):
            link[0] += 1
            ins.then_inc(link_sem, 1)
            dve.wait_ge(link_sem, link[0])

        linked(nc.vector.memset(mv[:, :, :, :], 1.0))

        def stats_of(b, tiles):
            for src, rows, k in tiles:
                last = nc.vector.bn_stats(stats[0:rows, b, k, :], src)
            linked(last)
            for src, rows, k in tiles:
                last = nc.vector.bn_aggr(mv[0:rows, b, k, :], stats[0:rows, b, k, :])
            return last

        def normed(b, tiles):
            linked(nc.vector.reciprocal(sd[:, b, 0:len(tiles)], sd[:, b, 0:len(tiles)]))
            for src, rows, k in tiles:
                last = nc.vector.tensor_scalar(src, src, mv[0:rows, b, k, 0:1], sd[0:rows, b, k:k + 1],
                                               ALU.subtract, ALU.mult)
            return last

        lat = [[(x_tok[:, QT * b + t, :], P, t) for t in range(QT)] for b in range(B)]
        con = [[(c_tok[:, b, 0, :], P, QT), (c_tok[0:REM, b, 1, :], REM, QT + 1)] for b in range(B)]
        dve.wait_ge(ld_x, 16)
        dve.wait_ge(ld_c, 32)
        for b in range(B):
            stats_of(b, lat[b] + con[b]).then_inc(var_ready, 1)
        for b in range(B):
            dve.wait_ge(sd_ready, b + 1)
            linked(normed(b, lat[b] + con[b]))
        for b in range(B):
            stats_of(b, lat[b]).then_inc(var_ready, 1)
        for b in range(B):
            dve.wait_ge(sd_ready, 2 + b + 1)
            normed(b, lat[b]).then_inc(rows_normed, 1)
        dve.wait_ge(pre_pool, PREP_MASK)

        for b in range(B):
            dve.wait_ge(pre_pe, 2 * b + 1)
            linked(nc.vector.tensor_scalar(kvT[:, b, C_LAT:C_LAT + S], psM[:, 512 * b:512 * b + S],
                                           gb[:, 2:3], gb[:, 3:4], ALU.mult, ALU.add))
            dve.wait_ge(pre_pe, 2 * b + 2)
            cT = kvT[:, b, C_LAT - P - RW:C_LAT]
            src = psT[:, 512 * b:512 * b + P + RW]
            linked(nc.vector.tensor_scalar(cT, src, gb[:, 0:1], gb[:, 1:2], ALU.mult, ALU.add))
            linked(nc.vector.tensor_scalar(lat0[:, b, :], lat0[:, b, :], kvT[:, b, C_LAT:C_LAT + 1], None, ALU.mult))
            linked(nc.vector.tensor_tensor(cT[:, RW:], cT[:, RW:], valid[:, b, 0:P], ALU.mult))
            linked(nc.vector.tensor_tensor(cT[:, 0:RW], cT[:, 0:RW], valid[:, b, P:], ALU.mult))
            linked(nc.vector.tensor_tensor(cT[:, RW:], cT[:, RW:], lat0[:, b, 0:P], ALU.add))
            linked(nc.vector.tensor_tensor(cT[:, 0:RW], cT[:, 0:RW], lat0[:, b, P:], ALU.add))
            nc.vector.tensor_copy(kvT[:, b, C_REM2:C_REM2 + RW], cT[:, 0:RW])
            nc.vector.tensor_copy(kvT[:, b, C_REM2 + RW:], cT[:, 0:RW]).then_inc(kv_ready, 1)

        def qk_low(u, nb):
            for h in range(2):
                dve.wait_ge(q_hi, 2 * u + h + 1)
                last = nc.vector.tensor_tensor(QA[nb][DH:P, h, :], psM[DH * h:DH * h + DH, 0:S],
                                               QA[nb][0:DH, h, :].bitcast(F32), ALU.subtract)
            last.then_inc(q_lo, 1)
            for h in range(2):
                dve.wait_ge(k_hi, 2 * u + h + 1)
                cols = slice(RW * h, RW * h + KEYS)
                src = psJ[DH * h:DH * h + DH, (RW if h == 0 else 0):][:, 0:KEYS]
                last = nc.vector.tensor_tensor(KB[nb][0:DH, h, cols], src, KA[nb][0:DH, h, cols].bitcast(F32),
                                               ALU.subtract)
            last.then_inc(k_lo, 1)

        def norm_out(u):
            dve.wait_ge(den_done, u + 1)
            nc.vector.reciprocal(rden[:, :], psX[:, :]).then_inc(rden_done, 1)
            dve.wait_ge(rden_done, u + 1)
            dve.wait_ge(o_out, u + 1)
            nc.vector.tensor_tensor(on[:, :], oraw[:, :], rden[:, :], ALU.mult).then_inc(on_done, 1)

        def maxima(u, ns):
            for n in ns:
                dve.wait_ge(sm_done, u * 2 * QT + n + 1)
                nc.vector.tensor_reduce(nm[:, n % QT, n // QT:n // QT + 1], psMJ[n % 2][:, :, 0:HALF], AX.XY, ALU.max,
                                        negate=True).then_inc(max_done, 1)

        def split_max(u):
            dve.wait_ge(max_done, (u + 1) * 2 * QT)
            nc.vector.tensor_copy(nmp[:, :, :, 0], nm[:, :, :]).then_inc(m_hi, 1)
            dve.wait_ge(m_hi, u + 1)
            nc.vector.tensor_tensor(nmp[:, :, :, 1], nm[:, :, :], nmp[:, :, :, 0], ALU.subtract).then_inc(m_split, 1)

        def add_out(u, b):
            dve.wait_ge(wo_done, u + 1)
            nc.vector.tensor_tensor(acc[:, b, :], acc[:, b, :], psX[:, :], ALU.add).then_inc(acc_done, 1)

        def unit(i, b, prev=True, nxt=True):
            u = 2 * i + b
            if nxt:
                qk_low(u + 1, 1 - b)
            if prev:
                norm_out(u - 1)
            if nxt:
                maxima(u + 1, range(0, 3))
            if prev:
                add_out(u - 1, 1 - b)
            if nxt:
                maxima(u + 1, range(3, 2 * QT))
                split_max(u + 1)

        qk_low(0, 0)
        maxima(0, range(2 * QT))
        split_max(0)
        dve.wait_ge(ld_w, 16)
        unit(0, 0, prev=False)
        unit(0, 1)
        with dve.Fori(1, PAIRS - 1) as i:
            unit(i, 0)
            unit(i, 1)
        unit(PAIRS - 1, 0)
        unit(PAIRS - 1, 1, nxt=False)

        def gate_groups(b):
            dve.wait_ge(scores_done, b + 1)
            linked(nc.vector.tensor_tensor(sm_[:, :, :], sc[:, :, :], gbias[:, :].unsqueeze(1).broadcast_to([P, QT, E_N]),
                                           ALU.add))
            sg = sm_[:, :, :].rearrange("p t (g e) -> p t g e", g=GROUPS)
            linked(nc.vector.tensor_reduce(gmx[:, :, :], sg, AX.X, ALU.max))
            other = gmx[:, :, :].unsqueeze(2).broadcast_to([P, QT, GROUPS, GROUPS])
            mine = gmx[:, :, :].unsqueeze(3).broadcast_to([P, QT, GROUPS, GROUPS])
            nc.vector.tensor_tensor(cmp_g[:, :, :, :], other, mine, ALU.is_gt)
            linked(nc.vector.tensor_tensor(eq_g[:, :, :, :], other, mine, ALU.is_equal))
            low = low4[:, :, :].unsqueeze(1).broadcast_to([P, QT, GROUPS, GROUPS])
            linked(nc.vector.tensor_tensor(eq_g[:, :, :, :], eq_g[:, :, :, :], low, ALU.mult))
            linked(nc.vector.tensor_tensor(cmp_g[:, :, :, :], cmp_g[:, :, :, :], eq_g[:, :, :, :], ALU.add))
            linked(nc.vector.tensor_reduce(keep[:, :, :], cmp_g[:, :, :, :], AX.X, ALU.add))
            linked(nc.vector.tensor_scalar(keep[:, :, :], keep[:, :, :], float(TOPK_GROUPS), None, ALU.is_lt))
            kb = keep[:, :, :].unsqueeze(3).broadcast_to([P, QT, GROUPS, GE])
            linked(nc.vector.tensor_tensor(sg, sg, kb, ALU.mult))
            linked(nc.vector.tensor_scalar(keep[:, :, :], keep[:, :, :], -1.0, BIG, ALU.add, ALU.mult))
            linked(nc.vector.tensor_tensor(sg, sg, kb, ALU.add))

        def gate_experts():
            for t in range(QT):
                last = nc.vector.max(top8[:, t, :], sm_[:, t, :])
            linked(last)
            fourth = top8[:, :, TOPK - 1:TOPK].broadcast_to([P, QT, E_N])
            nc.vector.tensor_tensor(more[:, :, :], sm_[:, :, :], fourth, ALU.is_gt)
            linked(nc.vector.tensor_tensor(same[:, :, :], sm_[:, :, :], fourth, ALU.is_equal))
            nc.vector.tensor_reduce(left[:, :, :], more[:, :, :], AX.X, ALU.add)
            linked(nc.vector.tensor_tensor_scan(nth[:, :, :].rearrange("p t e -> p (t e)"),
                                                again[:, :, :].rearrange("p t e -> p (t e)"),
                                                same[:, :, :].rearrange("p t e -> p (t e)"), 0.0, ALU.mult, ALU.add))
            linked(nc.vector.tensor_tensor(nth[:, :, :], nth[:, :, :], left[:, :, :].broadcast_to([P, QT, E_N]), ALU.add))
            linked(nc.vector.tensor_scalar(nth[:, :, :], nth[:, :, :], float(TOPK), None, ALU.is_le))
            linked(nc.vector.tensor_tensor(same[:, :, :], same[:, :, :], nth[:, :, :], ALU.mult))
            linked(nc.vector.tensor_tensor(more[:, :, :], more[:, :, :], same[:, :, :], ALU.add))
            nc.vector.tensor_tensor(comb[:, :, :], sc[:, :, :], more[:, :, :], ALU.mult).then_inc(comb_done, 1)

        def norm_tokens(b):
            dve.wait_ge(x2_turned, b + 1)
            src = turn_bank(b)
            tiles = [(src[:, P * t:P * t + P], P, t) for t in range(QT)]
            stats_of(b, tiles).then_inc(x2_stats, 1)
            dve.wait_ge(x2_sd, b + 1)
            linked(nc.vector.reciprocal(sd[:, b, 0:QT], sd[:, b, 0:QT]))
            for s_, rows, k in tiles:
                last = nc.vector.tensor_scalar(x2n[:, k, :], s_, mv[:, b, k, 0:1], sd[:, b, k:k + 1],
                                               ALU.subtract, ALU.mult)
            last.then_inc(x2_normed, 1)

        def spread_parts(b):
            dve.wait_ge(comb_turned, b + 1)
            src = back_bank(b)[0:E_N, 0:S]
            linked(nc.vector.tensor_copy(cparts[b][0:E_N, :], src))
            linked(nc.vector.tensor_tensor(cres[:, :], src, cparts[b][0:E_N, :], ALU.subtract))
            linked(nc.vector.tensor_copy(cparts[b][32:32 + E_N, :], cres[:, :]))
            nc.vector.tensor_tensor(cparts[b][64:64 + E_N, :], cres[:, :], cparts[b][32:32 + E_N, :], ALU.subtract)\
                .then_inc(parts_done, 1)

        def hidden(g):
            b, c = divmod(g, CH + 1)
            rows = P if c < CH else INTER
            dve.wait_ge(sil_done, g + 1)
            if g >= 2:
                dve.wait_ge(y_done, g - 1)
            h3 = psJ[0:rows, (g % 2) * 512:(g % 2) * 512 + S]
            h = hT[g % 2][0:rows, :]
            if c == CH:
                nc.vector.tensor_tensor(h, sil[g % 2][0:rows, :], h3, ALU.mult).then_inc(h_done, 1)
                return
            nc.vector.tensor_tensor(h, sil[g % 2][0:rows, :], h3, ALU.mult).then_inc(h_part, 1)
            dve.wait_ge(h_part, g - b + 1)
            dve.wait_ge(cb_done, g - b + 1)
            nc.vector.tensor_tensor(h, h, psT[:, (g % 2) * 512:(g % 2) * 512 + S], ALU.mult).then_inc(h_done, 1)

        def result(b):
            dve.wait_ge(y_done, (b + 1) * (CH + 1))
            nc.vector.tensor_tensor(res[:, b, :], acc[:, b, :], psO[:, :], ALU.add).then_inc(res_done, 1)

        dve.wait_ge(ld_f, 16 * 7)
        linked(nc.vector.tensor_copy(sel_b[:, :], sel_f[:, :]))
        norm_tokens(0)
        norm_out(UNITS - 1)
        add_out(UNITS - 1, 1)
        gate_groups(0)
        gate_experts()
        spread_parts(0)
        hidden(0)
        hidden(1)
        norm_tokens(1)
        hidden(2)
        hidden(3)
        gate_groups(1)
        hidden(4)
        gate_experts()
        hidden(5)
        spread_parts(1)
        hidden(6)
        for g in range(7, 2 * (CH + 1)):
            hidden(g)
            if g == CH:
                result(0)
        result(1)

    @block.tensor
    def _(pe):
        pe.wait_ge(ld_s, 16 * LD_S)
        for b in range(B):
            pe.wait_ge(rows_normed, b + 1)
            for t in range(QT):
                last = nc.tensor.transpose(psM[:, 512 * b + P * t:512 * b + P * t + P], x_tok[:, QT * b + t, :], idf[:, :])
            last.then_inc(pre_pe, 1)
            nc.tensor.transpose(psT[:, 512 * b:512 * b + RW], c_tok[0:RW, b, 1, :], idf[0:RW, 0:RW])
            nc.tensor.transpose(psT[:, 512 * b + RW:512 * b + RW + P], c_tok[:, b, 0, :], idf[:, :]).then_inc(pre_pe, 1)

        def project_k(b):
            for lo, hi in ((0, 512), (512, C_MAIN + MAIN + RW)):
                last = nc.tensor.matmul(psJ[:, lo:hi], wq[:, 1, :], kvT[:, b, lo:hi], start=True, stop=True)
            last.then_inc(k_done, 1)

        def project_q(b):
            nc.tensor.matmul(psM[:, 0:S], wq[:, 0, :], kvT[:, b, C_LAT:C_LAT + S], start=True, stop=True)\
                .then_inc(q_done, 1)

        def project_v(u, b):
            pe.wait_ge(k_lo, u + 1)
            for t in range(KT):
                nc.tensor.matmul(psJ[:, P * t:P * t + P], kvT[:, b, C_MAIN + P * t:C_MAIN + P * t + P], wq[:, 2, :],
                                 start=True, stop=True)
            nc.tensor.matmul(psJ[0:2 * RW, MAIN:MAIN + P], kvT[:, b, C_REM2:C_REM2 + 2 * RW], wq[:, 2, :],
                             start=True, stop=True).then_inc(v_done, 1)

        def max_scores(u, b, n):
            h, t = divmod(n, QT)
            if n == 0:
                pe.wait_ge(q_lo, u + 1)
                pe.wait_ge(k_lo, u + 1)
                pe.wait_ge(k_copied, u + 1)
            elif n == 1:
                pe.wait_ge(v_out, u + 1)
            else:
                pe.wait_ge(max_done, u * 2 * QT + n - 1)
            for a in range(2):
                lo = RW * h + HALF * a
                last = nc.tensor.matmul((psM, psJ)[n % 2][:, 512 * a:512 * a + HALF], QA[b][:, h, P * t:P * t + P],
                                        KA[b][:, h, lo:lo + HALF], start=True, stop=True)
            last.then_inc(sm_done, 1)

        def max_rows(u, b):
            pe.wait_ge(m_split, u + 1)
            for t in range(QT):
                last = nc.tensor.matmul(psX[DH:DH + 4, P * t:P * t + P], nmp[:, t, :, :].rearrange("p h a -> p (h a)"),
                                        idb[:, :], start=True, stop=True)
            last.then_inc(mrow_done, 1)

        def score_tile(u, b, n):
            bank = (b * STU + n) % 2
            dst = psT[:, bank * 512:bank * 512 + S]
            if n == 0:
                pe.wait_ge(m_out, u + 1)
                parts = [(0, MAIN), (1, 0)]
            else:
                if n >= 2:
                    pe.wait_ge(exp_done, u * STU + n - 1)
                h = (n - 1) % 2
                parts = [(h, RW * 2 * h + (n - 1) // 2 * P)]
            for j, (h, lo) in enumerate(parts):
                nc.tensor.matmul(dst, KA[b][:, h, lo:lo + P], QA[b][:, h, :], start=j == 0, stop=False)
                last = nc.tensor.matmul(dst, KB[b][:, h, lo:lo + P], QB[b][:, h, :], start=False, stop=j == len(parts) - 1)
            last.then_inc(st_done, 1)

        def weigh_values(u, b, j, prev=True):
            if j == 0:
                if prev:
                    pe.wait_ge(o_out, u)
                pe.wait_ge(v_out, u + 1)
            for h in range(2):
                cols = slice(DH * h, DH * h + DH)
                pe.wait_ge(exp_done, u * STU + (1 if j == 0 else 2 * j + h))
                if j == 0:
                    v, p = VR[b][:, cols], PRr[b][:, :]
                else:
                    v, p = V[b][:, j - 1, cols], PR[b][:, j - 1, h, :]
                last = nc.tensor.matmul(psO[cols, :], v, p, start=j == 0, stop=j == KT)
            if j == KT:
                last.then_inc(pv_done, 1)

        def denominators(u, b):
            pe.wait_ge(sum_done, u + 1)
            for h in range(2):
                last = nc.tensor.matmul(psX[DH * h:DH * h + DH, :], ones[:, :], SUM[b][:, h, :], start=True, stop=True)
            last.then_inc(den_done, 1)

        def project_out(u):
            pe.wait_ge(on_done, u + 1)
            nc.tensor.matmul(psX[:, :], wop[:, :], on[:, :], start=True, stop=True).then_inc(wo_done, 1)

        def unit(i, b, prev=True, nxt=True, first_pair=False):
            u = 2 * i + b
            if nxt:
                if b == 1:
                    pe.wait_ge(ld_qkv, 16 * (i + 2))
                pe.wait_ge(max_done, u * 2 * QT + 2 * QT - 1)
                project_q(1 - b)
            if not first_pair:
                pe.wait_ge(acc_done, u - 1)
            max_rows(u, b)
            if nxt:
                project_k(1 - b)
            score_tile(u, b, 0)
            score_tile(u, b, 1)
            if prev:
                denominators(u - 1, 1 - b)
            score_tile(u, b, 2)
            score_tile(u, b, 3)
            weigh_values(u, b, 0, prev)
            if nxt:
                project_v(u + 1, 1 - b)
            score_tile(u, b, 4)
            if nxt:
                max_scores(u + 1, 1 - b, 0)
            score_tile(u, b, 5)
            weigh_values(u, b, 1)
            weigh_values(u, b, 2)
            score_tile(u, b, 6)
            if nxt:
                max_scores(u + 1, 1 - b, 1)
            score_tile(u, b, 7)
            if nxt:
                max_scores(u + 1, 1 - b, 2)
            if prev:
                if b == 1:
                    pe.wait_ge(ld_wo, 16 * (i + 1))
                project_out(u - 1)
            if nxt:
                max_scores(u + 1, 1 - b, 3)
            score_tile(u, b, 8)
            if nxt:
                max_scores(u + 1, 1 - b, 4)
            score_tile(u, b, 9)
            if nxt:
                max_scores(u + 1, 1 - b, 5)
            weigh_values(u, b, 3)
            weigh_values(u, b, 4)
            score_tile(u, b, 10)
            if nxt:
                max_scores(u + 1, 1 - b, 6)
                max_scores(u + 1, 1 - b, 7)
            weigh_values(u, b, 5)

        pe.wait_ge(kv_ready, 1)
        pe.wait_ge(consts_ready, 1)
        pe.wait_ge(ld_qkv, 16)
        project_q(0)
        project_k(0)
        project_v(0, 0)
        for n in range(2 * QT):
            max_scores(0, 0, n)
        pe.wait_ge(kv_ready, 2)
        unit(0, 0, prev=False, first_pair=True)
        unit(0, 1, first_pair=True)
        with pe.Fori(1, PAIRS - 1) as i:
            unit(i, 0)
            unit(i, 1)
        unit(PAIRS - 1, 0)
        unit(PAIRS - 1, 1, nxt=False)

        def turn(b):
            for t in range(QT):
                last = nc.tensor.transpose(turn_bank(b)[:, P * t:P * t + P], acc[:, b, P * t:P * t + P], idf[:, :])
            last.then_inc(x2_turned, 1)

        def turn_back(b):
            pe.wait_ge(x2_normed, b + 1)
            for t in range(QT):
                last = nc.tensor.transpose(back_bank(b)[:, P * t:P * t + P], x2n[:, t, :], idf[:, :])
            last.then_inc(x2_back, 1)

        def gate(b):
            pe.wait_ge(x2_ready, b + 1)
            for t in range(QT):
                last = nc.tensor.matmul(turn_bank(b)[:, E_N * t:E_N * t + E_N], x2T[:, b, P * t:P * t + P], gw[:, :],
                                        start=True, stop=True)
            last.then_inc(gate_logits, 1)

        def turn_comb(b):
            pe.wait_ge(comb_done, b + 1)
            for t in range(QT):
                last = nc.tensor.transpose(back_bank(b)[0:E_N, P * t:P * t + P], comb[:, t, :], idf[:, :])
            last.then_inc(comb_turned, 1)

        def up(g):
            b, c = divmod(g, CH + 1)
            rows = P if c < CH else INTER
            if g >= 2:
                pe.wait_ge(h_done, g - 1)
            for w, bank in ((w1s, psM), (w3s, psJ)):
                last = nc.tensor.matmul(bank[0:rows, (g % 2) * 512:(g % 2) * 512 + S], w[:, P * c:P * c + rows],
                                        x2T[:, b, :], start=True, stop=True)
            last.then_inc(up_done, 1)

        def spread(g):
            b, c = divmod(g, CH + 1)
            if c < CH:
                nc.tensor.matmul(psT[:, (g % 2) * 512:(g % 2) * 512 + S], sel_b[:, P * c:P * c + P], cparts[b][:, :],
                                 start=True, stop=True).then_inc(cb_done, 1)

        def down(g):
            b, c = divmod(g, CH + 1)
            rows = P if c < CH else INTER
            if g == CH + 1:
                pe.wait_ge(res_done, 1)
            pe.wait_ge(h_done, g + 1)
            nc.tensor.matmul(psO[:, :], w2s[0:rows, c, :], hT[g % 2][0:rows, :], start=c == 0, stop=c == CH)\
                .then_inc(y_done, 1)

        pe.wait_ge(acc_done, UNITS - 1)
        turn(0)
        denominators(UNITS - 1, 1)
        turn_back(0)
        pe.wait_ge(ld_f, 16 * 7)
        gate(0)
        project_out(UNITS - 1)
        pe.wait_ge(scores_done, 1)
        up(0)
        pe.wait_ge(acc_done, UNITS)
        turn(1)
        turn_comb(0)
        pe.wait_ge(parts_done, 1)
        up(1)
        pe.wait_ge(parts_done, 1)
        spread(0)
        spread(1)
        down(0)
        for g in range(2, 2 * (CH + 1)):
            up(g)
            if g == CH + 1:
                pe.wait_ge(parts_done, 2)
            spread(g)
            down(g - 1)
            if g == 2:
                turn_back(1)
                gate(1)
            if g == 6:
                turn_comb(1)
        down(2 * (CH + 1) - 1)


def kernel(x, ctx_1024, mask_BxS2_bf1, L0_xattn_gm, L0_xattn_bm, L0_xattn_gl, L0_xattn_bl, L0_xattn_Wq, L0_xattn_Wk,
           L0_xattn_Wv, L0_xattn_Wo, L0_ffn_gate_w, L0_ffn_gate_bias, L0_ffn_w1, L0_ffn_w2, L0_ffn_w3, L0_ffn_ws1,
           L0_ffn_ws2, L0_ffn_ws3):
    import concourse.bacc as bacc
    import numpy as np
    from concourse.bass_utils import run_bass_kernel_spmd

    a = np.asarray
    xt = a(x).reshape(B * S, D)

    def by_pair(w):
        return a(w).reshape(D, PAIRS, P)

    own = np.zeros((4, 2, KEYS), np.float32)
    own[0:2, 0], own[2:4, 1] = 1.0, 1.0
    sel = np.zeros((80, CH * P), np.float32)
    for part in range(3):
        for e in range(E_N):
            sel[32 * part + e, e * INTER:(e + 1) * INTER] = 1.0
    arrays = {
        "xt": xt,
        "xT": xt.T,
        "cx": a(ctx_1024),
        "mask": a(mask_BxS2_bf1).view(np.uint8),
        "lngb": np.stack([a(L0_xattn_gm), a(L0_xattn_bm), a(L0_xattn_gl), a(L0_xattn_bl)], axis=1),
        "wqkv": np.stack([by_pair(L0_xattn_Wq), by_pair(L0_xattn_Wk), by_pair(L0_xattn_Wv)], axis=2).transpose(1, 0, 2, 3),
        "wo": a(L0_xattn_Wo).reshape(PAIRS, P, D),
        "gate_w": a(L0_ffn_gate_w).T,
        "gate_b": a(L0_ffn_gate_bias),
        "w1": np.concatenate([a(L0_ffn_w1).transpose(2, 0, 1).reshape(D, E_N * INTER), a(L0_ffn_ws1).T], axis=1),
        "w3": np.concatenate([a(L0_ffn_w3).transpose(2, 0, 1).reshape(D, E_N * INTER), a(L0_ffn_ws3).T], axis=1),
        "w2": a(L0_ffn_w2).transpose(0, 2, 1).reshape(E_N * INTER, D),
        "ws2": a(L0_ffn_ws2).T,
        "ident": np.eye(P, dtype=np.float32),
        "sel": sel,
        "own": own,
    }
    arrays = {"in_" + k: np.ascontiguousarray(v) for k, v in arrays.items()}
    nc = bacc.Bacc("TRN2", target_bir_lowering=False, num_devices=1)
    aps = [nc.dram_tensor(k, v.shape, mybir.dt.from_np(v.dtype), kind="ExternalInput").ap() for k, v in arrays.items()]
    out = nc.dram_tensor("out_T", (D, B * S), F32, kind="ExternalOutput").ap()
    with ExitStack() as ctx:
        build(nc, ctx, *aps, out)
    got = run_bass_kernel_spmd(nc, [arrays], core_ids=[0]).results[0]["out_T"]
    return np.ascontiguousarray(got.T).reshape(B, S, D)
```

```python
from contextlib import ExitStack

import concourse.bass as bass
from concourse import mybir

F32 = mybir.dt.float32
F32R = mybir.dt.float32r
BF16 = mybir.dt.bfloat16
U8 = mybir.dt.uint8
ACT = mybir.ActivationFunctionType
ALU = mybir.AluOpType
AX = mybir.AxisListType

P = 128
B, S, D = 2, 512, 128
CTX = 154
HEADS, DH = 16, 64
PAIRS = HEADS // 2
UNITS = B * PAIRS
SCALE = DH ** -0.5
EPS = 1e-5
QT = S // P
REM = CTX - P
RW = 32
MAIN = P + S
KT = MAIN // P
KEYS = MAIN + RW
HALF = KEYS // 2
C_MAIN, C_LAT, C_REM2 = RW, RW + P, RW + MAIN
KC = C_REM2 + RW
K_AT = 2 * P
C_ALL = C_REM2 + 2 * RW
E_N, INTER = 16, 64
GROUPS, TOPK_GROUPS, TOPK = 4, 2, 4
GE = E_N // GROUPS
CH = E_N * INTER // P
W13 = (E_N + 1) * INTER
CHUNKS = [(0, c) for c in range(CH + 1)] + [(1, CH)] + [(1, c) for c in range(CH)]
NCH = CH + 1
BIG = 1e30
STU = 1 + 2 * KT


def build(nc, ctx, xt, xT, cx, mask, maskT, lngb, wqkv, wo, gate_w, gate_b, w1, w3, w2, ws2, ident, sel, own, out):
    def sb(name, shape, dt=F32):
        return ctx.enter_context(nc.sbuf_tensor(name, shape, dt))

    def sem(name):
        return ctx.enter_context(nc.semaphore(name))

    x_tok = sb("x_tok", [P, B * QT, D])
    c_tok = sb("c_tok", [P, B, 2, D])
    acc = sb("acc", [P, B, S])
    gb = sb("gb", [P, 4])
    mrow_u8 = sb("mrow_u8", [P, B, CTX], U8)
    mcol_u8 = sb("mcol_u8", [P, 2, B], U8)
    valid = sb("valid", [P, B, RW + P])
    lat0 = sb("lat0", [P, B, RW + P])
    kbias = sb("kbias", [P, 2, B])
    idf = sb("idf", [P, P])
    idb = sb("idb", [P, P], BF16)
    ones = sb("ones", [P, DH])
    eps = sb("eps", [P, 1])
    warm = sb("warm", [P, 1])
    stats = sb("stats", [P, B, 6, 6])
    mv = sb("mv", [P, B, 6, 2])
    sd = sb("sd", [P, B, 6])
    kvT = sb("kvT", [P, B, C_ALL])
    kv_hi = sb("kv_hi", [P, B, KC], F32R)
    kv_lo = sb("kv_lo", [P, B, KC], F32R)
    wq = sb("wq", [P, 3, P])
    wq_hi = sb("wq_hi", [P, 2, P], F32R)
    wq_lo = sb("wq_lo", [P, 2, P], F32R)
    wop = sb("wop", [P, D])
    QA = [sb(f"QA{u}", [P, 2, S], F32R) for u in range(2)]
    QB = [sb(f"QB{u}", [DH + 4, 2, S], F32R) for u in range(2)]
    KA = [sb(f"KA{u}", [P, 2, MAIN + P], F32R) for u in range(2)]
    KB = [sb(f"KB{u}", [DH + 4, 2, MAIN + P], F32R) for u in range(2)]
    V = [sb(f"V{u}", [P, KT, P]) for u in range(2)]
    VR = [sb(f"VR{u}", [P, P]) for u in range(2)]
    nm = sb("nm", [P, QT, 2])
    nmp = sb("nmp", [P, QT, 2, 2], BF16)
    PR = [sb(f"PR{u}", [P, KT, 2, S]) for u in range(2)]
    own_f = PR[0][:, :, :, :].rearrange("p k h s -> p (k h s)")[:, 0:2 * KEYS].rearrange("p (h n) -> p h n", h=2)
    PRr = [sb(f"PRr{u}", [P, S]) for u in range(2)]
    SUM = [sb(f"SUM{u}", [P, 2, S]) for u in range(2)]
    oraw = sb("oraw", [P, S])
    rden = sb("rden", [P, S])
    on = sb("on", [P, S])
    gw = sb("gw", [P, E_N])
    gbias = sb("gbias", [P, E_N])
    w1s = sb("w1s", [P, W13])
    w3s = sb("w3s", [P, W13])
    w13_hi = sb("w13_hi", [P, 2, W13], F32R)
    w13_lo = sb("w13_lo", [P, 2, W13], F32R)
    w2s = sb("w2s", [P, CH + 1, D])
    sel_r = sb("sel_r", [RW + E_N, CH * P], F32R)
    low4 = sb("low4", [P, GROUPS, GROUPS])
    again = sb("again", [P, QT, E_N])
    top8 = sb("top8", [P, QT, 8])
    more = sb("more", [P, QT, E_N])
    same = sb("same", [P, QT, E_N])
    nth = sb("nth", [P, QT, E_N])
    left = sb("left", [P, QT, 1])
    x2n = sb("x2n", [P, QT, D])
    x2T = sb("x2T", [P, B, S])
    sel_f = x2T[0:RW + E_N, :, :].rearrange("p b s -> p (b s)")
    x2_hi = sb("x2_hi", [P, B, S], F32R)
    x2_lo = sb("x2_lo", [P, B, S], F32R)
    sc = sb("sc", [P, QT, E_N])
    sm_ = sb("sm_", [P, QT, E_N])
    gmx = sb("gmx", [P, QT, GROUPS])
    cmp_g = sb("cmp_g", [P, QT, GROUPS, GROUPS])
    eq_g = sb("eq_g", [P, QT, GROUPS, GROUPS])
    keep = sb("keep", [P, QT, GROUPS])
    comb = sb("comb", [P, QT, E_N])
    cparts = [sb(f"cparts{b}", [RW + E_N, S], F32R) for b in range(B)]
    sil = [sb(f"sil{u}", [P, S]) for u in range(2)]
    hT = [sb(f"hT{u}", [P, S]) for u in range(3)]

    def pb(name, banks):
        return ctx.enter_context(nc.psum_tensor(name, [P, banks * 512], F32))

    psM = pb("psM", 2)
    psJ = pb("psJ", 2)
    psT = pb("psT", 2)
    psO = pb("psO", 1)
    psX = pb("psX", 1)
    psMJ = [t[:, :].rearrange("p (a n) -> p a n", a=2) for t in (psM, psJ)]

    ld_x, ld_c, ld_s, ld_k, ld_w, ld_f = (sem(n) for n in ("ld_x", "ld_c", "ld_s", "ld_k", "ld_w", "ld_f"))
    ld_qkv, ld_wo, ld_x1, ld_m, ld_mT, ld_sel = (sem(n) for n in ("ld_qkv", "ld_wo", "ld_x1", "ld_m", "ld_mT", "ld_sel"))
    mask_ready, rsd_ready, pool_normed, sel_ready, comb_hi = (
        sem(n) for n in ("mask_ready", "rsd_ready", "pool_normed", "sel_ready", "comb_hi"))
    bias_ready, con_normed = sem("bias_ready"), sem("con_normed")
    kv_high, kv_low, wq_high, wq_low = (sem(n) for n in ("kv_high", "kv_low", "wq_high", "wq_low"))
    ld_w13, w13_high, w13_low, x2_low = (sem(n) for n in ("ld_w13", "w13_high", "w13_low", "x2_low"))
    var_ready, sd_ready, pre_pe, pre_pool = sem("var_ready"), sem("sd_ready"), sem("pre_pe"), sem("pre_pool")
    rows_normed, kv_ready, consts_ready = sem("rows_normed"), sem("kv_ready"), sem("consts_ready")
    k_done, q_done, v_done = sem("k_done"), sem("q_done"), sem("v_done")
    sm_done, mrow_done, st_done, pv_done = sem("sm_done"), sem("mrow_done"), sem("st_done"), sem("pv_done")
    den_done, wo_done = sem("den_done"), sem("wo_done")
    rows_second = sem("rows_second")
    rows_first, o_out, q_hi, k_hi, k_copied, v_out, exp_done = (
        sem(n) for n in ("rows_first", "o_out", "q_hi", "k_hi", "k_copied", "v_out", "exp_done"))
    q_lo, k_lo, max_done, m_hi, m_split, rden_done, on_done, acc_done = (
        sem(n) for n in ("q_lo", "k_lo", "max_done", "m_hi", "m_split", "rden_done", "on_done", "acc_done"))
    sum_step, sum_done = sem("sum_step"), sem("sum_done")
    x2_turned, x2_back, gate_logits, comb_turned = (sem(n) for n in ("x2_turned", "x2_back", "gate_logits", "comb_turned"))
    x2_stats, x2_normed, comb_done, parts_done = (sem(n) for n in ("x2_stats", "x2_normed", "comb_done", "parts_done"))
    x2_sd, x2_ready, scores_done = sem("x2_sd"), sem("x2_ready"), sem("scores_done")
    up_done, cb_done, y_done = sem("up_done"), sem("cb_done"), sem("y_done")
    sil_done, h_part, h_done, res_done = sem("sil_done"), sem("h_part"), sem("h_done"), sem("res_done")
    stored = sem("stored")

    def turn_bank(b):
        return psM[:, 0:512] if b == 0 else psX[:, :]

    def sum_bank(b):
        return (psO, psX)[b][:, :]

    def routed(g):
        return g - sum(c == CH for _, c in CHUNKS[:g])

    def back_bank(b):
        return psM[:, 512:1024] if b == 0 else psX[:, :]

    lat = [[(x_tok[:, QT * b + t, :], P, t) for t in range(QT)] for b in range(B)]
    con = [[(c_tok[:, b, 0, :], P, QT), (c_tok[0:REM, b, 1, :], REM, QT + 1)] for b in range(B)]

    block = ctx.enter_context(nc.Block())

    PREP_POOL = 3 + 2 + 2 + 8 + 2
    TOK = B * QT

    @block.sync
    def _(sp):
        x_tiles = xt.rearrange("(t p) d -> p t d", p=P)
        sp.dma_start(x_tok[:, 0:QT, :], x_tiles[:, 0:QT, :]).then_inc(ld_x, 16)
        sp.dma_start(c_tok[:, :, 0, :], cx[:, 0:P, :].rearrange("b p d -> p b d")).then_inc(ld_c, 16)
        sp.wait_ge(pre_pool, 3)
        sp.dma_start(c_tok[0:REM, :, 1, :], cx[:, P:CTX, :].rearrange("b p d -> p b d")).then_inc(ld_c, 16)
        sp.dma_start(mrow_u8[:, :, :], mask.partition_broadcast(P)).then_inc(ld_m, 16)
        sp.dma_start(own_f[DH:DH + 4, :, :], own).then_inc(ld_k, 16)
        sp.dma_start(wq[:, :, :], wqkv[0]).then_inc(ld_qkv, 16)
        sp.dma_start(x_tok[:, QT:TOK, :], x_tiles[:, QT:TOK, :]).then_inc(ld_x1, 16)
        sp.dma_start(mcol_u8[:, 0, :], maskT[0:P, :]).then_inc(ld_mT, 16)
        for h in range(2):
            sp.dma_start(mcol_u8[RW * h:RW * h + REM, 1, :], maskT[P:CTX, :]).then_inc(ld_mT, 16)
        sp.dma_start(w1s[:, :], w1).then_inc(ld_w13, 16)
        sp.dma_start(w3s[:, :], w3).then_inc(ld_w13, 16)
        sp.dma_start(wop[:, :], wo[0]).then_inc(ld_wo, 16)
        sp.dma_start(acc[:, :, :], xT.rearrange("d (b s) -> d b s", b=B)).then_inc(ld_w, 16)
        sp.dma_start(sel_f, sel).then_inc(ld_sel, 16)
        sp.dma_start(gw[:, :], gate_w).then_inc(ld_f, 16)
        sp.dma_start(gbias[:, :], gate_b.partition_broadcast(P)).then_inc(ld_f, 16)
        sp.dma_start(w2s[:, 0:CH, :], w2.rearrange("(c p) d -> p c d", p=P)).then_inc(ld_f, 16)
        sp.dma_start(w2s[0:INTER, CH, :], ws2).then_inc(ld_f, 16)

        def load_qkv(u, src):
            sp.wait_ge(v_done, u)
            sp.dma_start(wq[:, :, :], src).then_inc(ld_qkv, 16)

        def load_wo(u, src):
            sp.wait_ge(wo_done, u)
            sp.dma_start(wop[:, :], src).then_inc(ld_wo, 16)

        def qkv_of(p):
            return wqkv[bass.ds(p, 1)].rearrange("o k n m -> (o k) n m")

        def wo_of(p):
            return wo[bass.ds(p, 1)].rearrange("o k n -> (o k) n")

        load_qkv(1, wqkv[1])
        load_qkv(2, wqkv[2])
        with sp.Fori(3, PAIRS) as u:
            load_qkv(u, qkv_of(u))
            load_wo(u - 2, wo_of(u - 2))
        load_qkv(PAIRS, wqkv[0])
        load_wo(PAIRS - 2, wo[PAIRS - 2])
        load_qkv(PAIRS + 1, wqkv[1])
        load_wo(PAIRS - 1, wo[PAIRS - 1])
        with sp.Fori(2, PAIRS) as p:
            load_qkv(p + PAIRS, qkv_of(p))
            load_wo(p + PAIRS - 2, wo_of(p - 2))
        load_wo(UNITS - 2, wo[PAIRS - 2])
        load_wo(UNITS - 1, wo[PAIRS - 1])
        for b in range(B):
            sp.wait_ge(res_done, b + 1)
            sp.dma_start(out[:, b * S:(b + 1) * S], acc[:, b, :]).then_inc(stored, 16)
        sp.wait_ge(stored, 16 * B)

    @block.gpsimd
    def _(pool):
        nc.gpsimd.memset(eps[:, :], EPS).then_inc(pre_pool, 1)
        nc.gpsimd.memset(c_tok[0:RW, :, 1, :], 0.0).then_inc(pre_pool, 1)
        nc.gpsimd.memset(mcol_u8[:, :, :], 0).then_inc(pre_pool, 1)
        nc.gpsimd.memset(low4[:, :, :], 1.0).then_inc(pre_pool, 1)
        nc.gpsimd.memset(again[:, :, :], 1.0).then_inc(pre_pool, 1)
        for u in range(2):
            nc.gpsimd.memset(VR[u][:, :], 0.0).then_inc(pre_pool, 1)
        for u in range(2):
            for t, rows in ((KA[u], P), (KB[u], DH + 4)):
                nc.gpsimd.memset(t[0:rows, 0, KEYS:].bitcast(F32), 0.0).then_inc(pre_pool, 1)
                nc.gpsimd.memset(t[0:rows, 1, 0:RW].bitcast(F32), 0.0).then_inc(pre_pool, 1)
        for u in range(2):
            nc.gpsimd.memset(cparts[u][:, :].bitcast(F32), 0.0).then_inc(pre_pool, 1)
        pool.wait_ge(pre_pool, PREP_POOL)
        nc.gpsimd.memset(ones[:, :], 1.0).then_inc(pre_pool, 1)
        nc.gpsimd.memset(again[:, :, 0:1], 0.0).then_inc(pre_pool, 1)
        nc.gpsimd.affine_select(out=low4[:, :, :], in_=low4[:, :, :], compare_op=ALU.is_gt, fill=0.0, base=0,
                                pattern=[[1, GROUPS], [-1, GROUPS]], channel_multiplier=0).then_inc(pre_pool, 1)
        pool.wait_ge(ld_m, 16)
        nc.gpsimd.tensor_copy(valid[:, :, RW:], mrow_u8[:, :, 0:P]).then_inc(mask_ready, 1)
        nc.gpsimd.tensor_copy(valid[:, :, 0:REM], mrow_u8[:, :, P:]).then_inc(mask_ready, 1)
        nc.gpsimd.memset(valid[:, :, REM:RW], 0.0).then_inc(mask_ready, 1)
        pool.wait_ge(mask_ready, 3)
        nc.gpsimd.tensor_scalar(lat0[:, :, :], valid[:, :, :], -1.0, 1.0, ALU.mult, ALU.add).then_inc(mask_ready, 1)
        pool.wait_ge(ld_mT, 16 * 3)
        nc.gpsimd.tensor_scalar(kbias[:, :, :], mcol_u8[:, :, :], -1.0, BIG, ALU.add, ALU.mult).then_inc(bias_ready, 1)
        for level in range(2):
            pool.wait_ge(rsd_ready, level + 1)
            for src, rows, k in lat[1]:
                nc.gpsimd.tensor_scalar(src, src, mv[0:rows, 1, k, 0:1], sd[0:rows, 1, k:k + 1],
                                        ALU.subtract, ALU.mult).then_inc(pool_normed, 1)

        def weights_low(u):
            pool.wait_ge(wq_high, u)
            nc.gpsimd.tensor_tensor(wq_lo[:, :, :], wq[:, 0:2, :], wq_hi[:, :, :].bitcast(F32), ALU.subtract)\
                .then_inc(wq_low, 1)

        def inputs_low(b):
            pool.wait_ge(kv_high, b + 1)
            nc.gpsimd.tensor_tensor(kv_lo[:, b, :], kvT[:, b, 0:KC], kv_hi[:, b, :].bitcast(F32), ALU.subtract)\
                .then_inc(kv_low, 1)

        def sums(u, par, split=True):
            step = u * 5
            s, pr, rest = SUM[par], PR[par], PRr[par]
            pool.wait_ge(exp_done, u * STU + 5)
            nc.gpsimd.tensor_tensor(s[:, :, :], pr[:, 0], pr[:, 1], ALU.add).then_inc(sum_step, 1)
            for h in range(2):
                pool.wait_ge(sum_step, step + 1 + h)
                r = slice(RW * h, RW * h + REM)
                nc.gpsimd.tensor_tensor(s[r, h, :], s[r, h, :], rest[r, :], ALU.add).then_inc(sum_step, 1)
            for t in range(2, KT):
                pool.wait_ge(exp_done, u * STU + 3 + 2 * t)
                pool.wait_ge(sum_step, step + 1 + t)
                nc.gpsimd.tensor_tensor(s[:, :, :], s[:, :, :], pr[:, t], ALU.add)\
                    .then_inc(sum_step if t < KT - 1 else sum_done, 1)
                if split and t == 2:
                    weights_low(u + 2)

        inputs_low(0)
        weights_low(1)
        for k, w in enumerate((w1s, w3s)):
            pool.wait_ge(w13_high, k + 1)
            nc.gpsimd.tensor_tensor(w13_lo[:, k, :], w[:, :], w13_hi[:, k, :].bitcast(F32), ALU.subtract)\
                .then_inc(w13_low, 1)
        sums(0, 0)
        inputs_low(1)
        sums(1, 1)
        with pool.Fori(1, PAIRS - 1) as i:
            sums(2 * i, 0)
            sums(2 * i + 1, 1)
        sums(UNITS - 2, 0, split=False)
        sums(UNITS - 1, 1, split=False)

    @block.scalar
    def _(act):
        act.wait_ge(pre_pool, 1)
        nc.scalar.activation(warm[:, :], eps[:, :], ACT.Sqrt)
        act.dma_start(idf[:, :], ident).then_inc(ld_s, 16)
        act.dma_start(gb[:, :], lngb).then_inc(ld_s, 16)

        def deviations(b, k0, k1, count):
            act.wait_ge(var_ready, count)
            nc.scalar.activation(sd[:, b, k0:k1], mv[:, b, k0:k1, 1], ACT.Sqrt, bias=eps[:, 0:1]).then_inc(sd_ready, 1)

        deviations(0, 0, QT, 1)
        deviations(0, QT, QT + 2, 2)
        deviations(0, 0, QT, 3)
        act.wait_ge(ld_s, 32)
        nc.scalar.activation(idb[:, :], idf[:, :], ACT.Copy)
        act.wait_ge(ld_k, 16)
        for u in range(2):
            for h in range(2):
                last = nc.scalar.activation(KB[u][DH:DH + 4, h, RW * h:RW * h + KEYS], own_f[DH:DH + 4, h, :], ACT.Copy)
            if u == 0:
                deviations(1, 0, QT + 2, 4)
        last.then_inc(consts_ready, 1)

        def q_high(u, nb):
            act.wait_ge(q_done, u + 1)
            for h in range(2):
                nc.scalar.activation(QA[nb][0:DH, h, :], psM[DH * h:DH * h + DH, 0:S], ACT.Copy).then_inc(q_hi, 1)

        def k_high(u, nb, h):
            if h == 0:
                act.wait_ge(k_done, u + 1)
            dst = KA[nb][0:DH, h, RW * h:RW * h + KEYS]
            src = psJ[DH * h:DH * h + DH, K_AT + (RW if h == 0 else 0):][:, 0:KEYS]
            nc.scalar.activation(dst, src, ACT.Copy).then_inc(k_hi, 1)

        def q_copy(u, nb, h):
            act.wait_ge(q_hi, 2 * u + h + 1)
            nc.scalar.activation(QB[nb][0:DH, h, :], QA[nb][0:DH, h, :].bitcast(F32), ACT.Copy)

        def k_copy(u, nb, h):
            act.wait_ge(k_hi, 2 * u + h + 1)
            dst = KA[nb][DH:P, h, RW * h:RW * h + KEYS]
            src = KA[nb][0:DH, h, RW * h:RW * h + KEYS]
            nc.scalar.activation(dst, src.bitcast(F32), ACT.Copy).then_inc(k_copied, 1)

        def v_copy(u, nb, bank):
            act.wait_ge(v_done, u + 1)
            nc.scalar.activation(V[nb][:, :, :].rearrange("p k n -> p (k n)"), bank[:, 0:KT * P], ACT.Copy)
            for h in range(2):
                r = slice(RW * h, RW * h + REM)
                last = nc.scalar.activation(VR[nb][r, DH * h:DH * h + DH],
                                            bank[r, KT * P + DH * h:KT * P + DH * h + DH], ACT.Copy)
            last.then_inc(v_out, 1)

        def exp_tile(u, par, b, n):
            act.wait_ge(st_done, u * STU + n + 1)
            bank = (par * STU + n) % 2
            src = psT[:, bank * 512:bank * 512 + S]
            if n == 0:
                last = nc.scalar.activation(PRr[par][:, :], src, ACT.Exp, bias=kbias[:, 1, b:b + 1],
                                            scale=SCALE)
            elif n <= 2:
                last = nc.scalar.activation(PR[par][:, 0, n - 1, :], src, ACT.Exp, bias=kbias[:, 0, b:b + 1], scale=SCALE)
            else:
                last = nc.scalar.activation(PR[par][:, (n - 1) // 2, (n - 1) % 2, :], src, ACT.Exp, scale=SCALE)
            last.then_inc(exp_done, 1)

        def o_copy(u):
            act.wait_ge(pv_done, u + 1)
            nc.scalar.activation(oraw[:, :], psO[:, :], ACT.Copy).then_inc(o_out, 1)

        def unit(u, par, b, prev=True, first=False, split=True):
            other = 1 - par
            act.wait_ge(mrow_done, u + 1)
            nc.scalar.activation(QB[par][DH:DH + 4, 0, :], psX[DH:DH + 4, :], ACT.Copy).then_inc(rows_first, 1)
            q_high(u + 1, other)
            if prev:
                if not first:
                    act.wait_ge(on_done, u - 1)
                o_copy(u - 1)
            k_high(u + 1, other, 0)
            exp_tile(u, par, b, 0)
            exp_tile(u, par, b, 1)
            k_high(u + 1, other, 1)
            exp_tile(u, par, b, 2)
            k_copy(u + 1, other, 1)
            k_copy(u + 1, other, 0)
            exp_tile(u, par, b, 3)
            exp_tile(u, par, b, 4)
            q_copy(u + 1, other, 0)
            v_copy(u + 1, other, psJ)
            exp_tile(u, par, b, 5)
            if split:
                weights_high(u + 2)
            exp_tile(u, par, b, 6)
            exp_tile(u, par, b, 7)
            exp_tile(u, par, b, 8)
            exp_tile(u, par, b, 9)
            q_copy(u + 1, other, 1)
            exp_tile(u, par, b, 10)

        def token_deviations(b):
            act.wait_ge(x2_stats, b + 1)
            nc.scalar.activation(sd[:, b, 0:QT], mv[:, b, 0:QT, 1], ACT.Sqrt, bias=eps[:, 0:1]).then_inc(x2_sd, 1)

        def tokens_back(b):
            act.wait_ge(x2_back, b + 1)
            nc.scalar.activation(x2_hi[:, b, :], back_bank(b)[:, 0:S], ACT.Copy)
            nc.scalar.activation(x2T[:, b, :], back_bank(b)[:, 0:S], ACT.Copy).then_inc(x2_ready, 1)

        def gate_exp(b):
            act.wait_ge(gate_logits, b + 1)
            nc.scalar.activation(sc[:, :, :].rearrange("p t e -> p (t e)"), turn_bank(b)[:, 0:QT * E_N], ACT.Exp,
                                 scale=-1.0).then_inc(scores_done, 1)

        def comb_high(b):
            act.wait_ge(comb_turned, b + 1)
            nc.scalar.activation(cparts[b][0:E_N, :], back_bank(b)[0:E_N, 0:S], ACT.Copy).then_inc(comb_hi, 1)

        def inputs_high(b):
            act.wait_ge(kv_ready, 2 * b + 2)
            nc.scalar.activation(kv_hi[:, b, :], kvT[:, b, 0:KC], ACT.Copy).then_inc(kv_high, 1)

        def weights_high(u):
            act.wait_ge(ld_qkv, 16 * (u + 1))
            act.wait_ge(k_done, u)
            nc.scalar.activation(wq_hi[:, :, :], wq[:, 0:2, :], ACT.Copy).then_inc(wq_high, 1)

        act.wait_ge(pre_pool, PREP_POOL)
        q_high(0, 0)
        inputs_high(0)
        k_high(0, 0, 0)
        k_high(0, 0, 1)
        k_copy(0, 0, 0)
        k_copy(0, 0, 1)
        deviations(1, 0, QT, 5)
        v_copy(0, 0, psT)
        q_copy(0, 0, 0)
        q_copy(0, 0, 1)
        weights_high(1)
        act.wait_ge(bias_ready, 1)
        nc.scalar.activation(warm[:, :], kbias[:, 0, 0:1], ACT.Exp)
        act.wait_ge(ld_w13, 32)
        for k, w in enumerate((w1s, w3s)):
            nc.scalar.activation(w13_hi[:, k, :], w[:, :], ACT.Copy).then_inc(w13_high, 1)
        unit(0, 0, 0, prev=False)
        inputs_high(1)
        unit(1, 1, 0, first=True)
        unit(2, 0, 0)
        with act.Fori(1, PAIRS // 2 - 1) as i:
            unit(2 * i + 1, 1, 0)
            unit(2 * i + 2, 0, 0)
        unit(PAIRS - 1, 1, 0)
        unit(PAIRS, 0, 1)
        with act.Fori(PAIRS // 2, PAIRS - 2) as i:
            unit(2 * i + 1, 1, 1)
            unit(2 * i + 2, 0, 1)
        unit(UNITS - 3, 1, 1)
        unit(UNITS - 2, 0, 1, split=False)
        act.wait_ge(mrow_done, UNITS)
        nc.scalar.activation(QB[1][DH:DH + 4, 0, :], psX[DH:DH + 4, :], ACT.Copy).then_inc(rows_first, 1)
        act.wait_ge(on_done, UNITS - 2)
        o_copy(UNITS - 2)
        token_deviations(0)
        exp_tile(UNITS - 1, 1, 1, 0)
        exp_tile(UNITS - 1, 1, 1, 1)
        exp_tile(UNITS - 1, 1, 1, 2)
        exp_tile(UNITS - 1, 1, 1, 3)
        tokens_back(0)
        exp_tile(UNITS - 1, 1, 1, 4)
        gate_exp(0)
        exp_tile(UNITS - 1, 1, 1, 5)
        exp_tile(UNITS - 1, 1, 1, 6)
        exp_tile(UNITS - 1, 1, 1, 7)
        exp_tile(UNITS - 1, 1, 1, 8)
        exp_tile(UNITS - 1, 1, 1, 9)
        exp_tile(UNITS - 1, 1, 1, 10)
        comb_high(0)
        act.wait_ge(on_done, UNITS - 1)
        o_copy(UNITS - 1)

        def silu(g):
            c = CHUNKS[g][1]
            rows = P if c < CH else INTER
            act.wait_ge(up_done, g + 1)
            if g >= 2:
                act.wait_ge(h_done, g - 1)
            nc.scalar.activation(sil[g % 2][0:rows, :], psM[0:rows, (g % 2) * 512:(g % 2) * 512 + S],
                                 ACT.Silu).then_inc(sil_done, 1)

        for g in range(len(CHUNKS)):
            silu(g)
            if g == 5:
                token_deviations(1)
            elif g == 6:
                tokens_back(1)
            elif g == 7:
                gate_exp(1)
            elif g == 9:
                comb_high(1)

    @block.vector
    def _(dve):
        link = [0]
        link_sem = sem("dve_link")

        def linked(ins):
            link[0] += 1
            ins.then_inc(link_sem, 1)
            dve.wait_ge(link_sem, link[0])

        linked(nc.vector.memset(mv[:, :, :, :], 1.0))

        def stats_of(b, tiles):
            for src, rows, k in tiles:
                last = nc.vector.bn_stats(stats[0:rows, b, k, :], src)
            linked(last)
            for src, rows, k in tiles:
                last = nc.vector.bn_aggr(mv[0:rows, b, k, :], stats[0:rows, b, k, :])
            return last

        def deviations_inverted(b, k0, k1, count):
            dve.wait_ge(sd_ready, count)
            return nc.vector.reciprocal(sd[:, b, k0:k1], sd[:, b, k0:k1])

        def centred(b, tiles):
            for src, rows, k in tiles:
                last = nc.vector.tensor_scalar(src, src, mv[0:rows, b, k, 0:1], sd[0:rows, b, k:k + 1],
                                               ALU.subtract, ALU.mult)
            return last

        def latents_turned(b, src):
            nc.vector.tensor_scalar(kvT[:, b, C_LAT:C_LAT + S], src, gb[:, 2:3], gb[:, 3:4], ALU.mult, ALU.add)\
                .then_inc(kv_ready, 1)

        def context_turned(b, src):
            cT = kvT[:, b, 0:C_LAT]
            linked(nc.vector.tensor_scalar(cT, src, gb[:, 0:1], gb[:, 1:2], ALU.mult, ALU.add))
            nc.vector.tensor_scalar(lat0[:, b, :], lat0[:, b, :], kvT[:, b, C_LAT:C_LAT + 1], None, ALU.mult)
            linked(nc.vector.tensor_tensor(cT, cT, valid[:, b, :], ALU.mult))
            linked(nc.vector.tensor_tensor(cT, cT, lat0[:, b, :], ALU.add))
            nc.vector.tensor_copy(kvT[:, b, C_REM2:].rearrange("p (a n) -> p a n", a=2),
                                  cT[:, 0:RW].unsqueeze(1).broadcast_to([P, 2, RW])).then_inc(kv_ready, 1)

        dve.wait_ge(ld_x, 16)
        stats_of(0, lat[0]).then_inc(var_ready, 1)
        dve.wait_ge(ld_c, 32)
        stats_of(0, con[0]).then_inc(var_ready, 1)
        linked(deviations_inverted(0, 0, QT, 1))
        linked(centred(0, lat[0]))
        stats_of(0, lat[0]).then_inc(var_ready, 1)
        linked(deviations_inverted(0, QT, QT + 2, 2))
        centred(0, con[0]).then_inc(rows_normed, 1)
        linked(deviations_inverted(0, 0, QT, 3))
        centred(0, lat[0]).then_inc(rows_normed, 1)
        dve.wait_ge(ld_x1, 16)
        stats_of(1, lat[1] + con[1]).then_inc(var_ready, 1)

        dve.wait_ge(ld_s, 32)
        dve.wait_ge(pre_pe, 2)
        latents_turned(0, psM[:, 0:S])
        deviations_inverted(1, 0, QT + 2, 4).then_inc(rsd_ready, 1)
        dve.wait_ge(mask_ready, 4)
        dve.wait_ge(kv_ready, 1)
        dve.wait_ge(rsd_ready, 1)
        context_turned(0, psT[:, 0:RW + P])
        centred(1, con[1]).then_inc(con_normed, 1)

        def q_low(u, nb):
            for h in range(2):
                dve.wait_ge(q_hi, 2 * u + h + 1)
                last = nc.vector.tensor_tensor(QA[nb][DH:P, h, :], psM[DH * h:DH * h + DH, 0:S],
                                               QA[nb][0:DH, h, :].bitcast(F32), ALU.subtract)
            last.then_inc(q_lo, 1)

        def k_low(u, nb):
            for h in range(2):
                dve.wait_ge(k_hi, 2 * u + h + 1)
                cols = slice(RW * h, RW * h + KEYS)
                src = psJ[DH * h:DH * h + DH, K_AT + (RW if h == 0 else 0):][:, 0:KEYS]
                last = nc.vector.tensor_tensor(KB[nb][0:DH, h, cols], src, KA[nb][0:DH, h, cols].bitcast(F32),
                                               ALU.subtract)
            last.then_inc(k_lo, 1)

        def norm_out(u):
            dve.wait_ge(den_done, u + 1)
            nc.vector.reciprocal(rden[:, :], psX[:, :]).then_inc(rden_done, 1)
            dve.wait_ge(rden_done, u + 1)
            dve.wait_ge(o_out, u + 1)
            nc.vector.tensor_tensor(on[:, :], oraw[:, :], rden[:, :], ALU.mult).then_inc(on_done, 1)

        def norm_last(k):
            dve.wait_ge(den_done, UNITS)
            dve.wait_ge(o_out, UNITS)
            half = slice(k * S // 2, (k + 1) * S // 2)
            linked(nc.vector.reciprocal(rden[:, half], psX[:, half]))
            last = nc.vector.tensor_tensor(on[:, half], oraw[:, half], rden[:, half], ALU.mult)
            if k == 1:
                last.then_inc(on_done, 1)

        def maxima(u, ns):
            for n in ns:
                dve.wait_ge(sm_done, u * 2 * QT + n + 1)
                nc.vector.tensor_reduce(nm[:, n % QT, n // QT:n // QT + 1], psMJ[n % 2][:, :, 0:HALF], AX.XY, ALU.max,
                                        negate=True).then_inc(max_done, 1)

        def split_max(u):
            dve.wait_ge(max_done, (u + 1) * 2 * QT)
            nc.vector.tensor_copy(nmp[:, :, :, 0], nm[:, :, :]).then_inc(m_hi, 1)
            dve.wait_ge(m_hi, u + 1)
            nc.vector.tensor_tensor(nmp[:, :, :, 1], nm[:, :, :], nmp[:, :, :, 0], ALU.subtract).then_inc(m_split, 1)

        def add_out(u, b):
            dve.wait_ge(wo_done, u + 1)
            nc.vector.tensor_tensor(acc[:, b, :], acc[:, b, :], psX[:, :], ALU.add).then_inc(acc_done, 1)

        def rows_out(u, par):
            dve.wait_ge(rows_first, u + 1)
            nc.vector.tensor_copy(QB[par][DH:DH + 4, 1, :], QB[par][DH:DH + 4, 0, :].bitcast(F32)).then_inc(rows_second, 1)

        def unit(u, par, pb, prev=True):
            other = 1 - par
            rows_out(u, par)
            q_low(u + 1, other)
            k_low(u + 1, other)
            if prev:
                norm_out(u - 1)
            else:
                dve.wait_ge(pre_pe, 3)
                latents_turned(1, psX[:, 0:S])
            maxima(u + 1, range(0, 5))
            if prev:
                add_out(u - 1, pb)
            else:
                dve.wait_ge(pre_pe, 4)
                dve.wait_ge(kv_ready, 3)
                context_turned(1, psX[:, 0:RW + P])
            maxima(u + 1, range(5, 2 * QT))
            split_max(u + 1)

        def token_stats(b):
            dve.wait_ge(x2_turned, b + 1)
            stats_of(b, turned_tiles(b)).then_inc(x2_stats, 1)

        def turned_tiles(b):
            return [(turn_bank(b)[:, P * t:P * t + P], P, t) for t in range(QT)]

        def token_norm(b):
            dve.wait_ge(x2_sd, b + 1)
            linked(nc.vector.reciprocal(sd[:, b, 0:QT], sd[:, b, 0:QT]))
            for src, rows, k in turned_tiles(b):
                last = nc.vector.tensor_scalar(x2n[:, k, :], src, mv[:, b, k, 0:1], sd[:, b, k:k + 1],
                                               ALU.subtract, ALU.mult)
            last.then_inc(x2_normed, 1)

        q_low(0, 0)
        dve.wait_ge(pool_normed, QT)
        stats_of(1, lat[1]).then_inc(var_ready, 1)
        k_low(0, 0)
        maxima(0, range(2))
        deviations_inverted(1, 0, QT, 5).then_inc(rsd_ready, 1)
        maxima(0, range(2, 2 * QT))
        split_max(0)
        dve.wait_ge(ld_w, 16)
        unit(0, 0, 0, prev=False)
        dve.wait_ge(ld_sel, 16)
        nc.vector.tensor_copy(sel_r[:, :], sel_f).then_inc(sel_ready, 1)
        unit(1, 1, 0)
        unit(2, 0, 0)
        with dve.Fori(1, PAIRS // 2 - 1) as i:
            unit(2 * i + 1, 1, 0)
            unit(2 * i + 2, 0, 0)
        unit(PAIRS - 1, 1, 0)
        unit(PAIRS, 0, 0)
        with dve.Fori(PAIRS // 2, PAIRS - 1) as i:
            unit(2 * i + 1, 1, 1)
            unit(2 * i + 2, 0, 1)

        def gate_groups(b):
            dve.wait_ge(scores_done, b + 1)
            linked(nc.vector.tensor_scalar(sc[:, :, :], sc[:, :, :], 1.0, None, ALU.add))
            linked(nc.vector.reciprocal(sc[:, :, :], sc[:, :, :]))
            linked(nc.vector.tensor_tensor(sm_[:, :, :], sc[:, :, :], gbias[:, :].unsqueeze(1).broadcast_to([P, QT, E_N]),
                                           ALU.add))
            sg = sm_[:, :, :].rearrange("p t (g e) -> p t g e", g=GROUPS)
            linked(nc.vector.tensor_reduce(gmx[:, :, :], sg, AX.X, ALU.max))
            other = gmx[:, :, :].unsqueeze(2).broadcast_to([P, QT, GROUPS, GROUPS])
            mine = gmx[:, :, :].unsqueeze(3).broadcast_to([P, QT, GROUPS, GROUPS])
            nc.vector.tensor_tensor(cmp_g[:, :, :, :], other, mine, ALU.is_gt)
            linked(nc.vector.tensor_tensor(eq_g[:, :, :, :], other, mine, ALU.is_equal))
            low = low4[:, :, :].unsqueeze(1).broadcast_to([P, QT, GROUPS, GROUPS])
            linked(nc.vector.tensor_tensor(eq_g[:, :, :, :], eq_g[:, :, :, :], low, ALU.mult))
            linked(nc.vector.tensor_tensor(cmp_g[:, :, :, :], cmp_g[:, :, :, :], eq_g[:, :, :, :], ALU.add))
            linked(nc.vector.tensor_reduce(keep[:, :, :], cmp_g[:, :, :, :], AX.X, ALU.add))
            linked(nc.vector.tensor_scalar(keep[:, :, :], keep[:, :, :], float(TOPK_GROUPS), None, ALU.is_lt))
            kb = keep[:, :, :].unsqueeze(3).broadcast_to([P, QT, GROUPS, GE])
            linked(nc.vector.tensor_tensor(sg, sg, kb, ALU.mult))
            linked(nc.vector.tensor_scalar(keep[:, :, :], keep[:, :, :], -1.0, BIG, ALU.add, ALU.mult))
            linked(nc.vector.tensor_tensor(sg, sg, kb, ALU.add))

        def gate_experts():
            for t in range(QT):
                last = nc.vector.max(top8[:, t, :], sm_[:, t, :])
            linked(last)
            fourth = top8[:, :, TOPK - 1:TOPK].broadcast_to([P, QT, E_N])
            nc.vector.tensor_tensor(more[:, :, :], sm_[:, :, :], fourth, ALU.is_gt)
            linked(nc.vector.tensor_tensor(same[:, :, :], sm_[:, :, :], fourth, ALU.is_equal))
            nc.vector.tensor_reduce(left[:, :, :], more[:, :, :], AX.X, ALU.add)
            linked(nc.vector.tensor_tensor_scan(nth[:, :, :].rearrange("p t e -> p (t e)"),
                                                again[:, :, :].rearrange("p t e -> p (t e)"),
                                                same[:, :, :].rearrange("p t e -> p (t e)"), 0.0, ALU.mult, ALU.add))
            linked(nc.vector.tensor_tensor(nth[:, :, :], nth[:, :, :], left[:, :, :].broadcast_to([P, QT, E_N]), ALU.add))
            linked(nc.vector.tensor_scalar(nth[:, :, :], nth[:, :, :], float(TOPK), None, ALU.is_le))
            linked(nc.vector.tensor_tensor(same[:, :, :], same[:, :, :], nth[:, :, :], ALU.mult))
            linked(nc.vector.tensor_tensor(more[:, :, :], more[:, :, :], same[:, :, :], ALU.add))
            nc.vector.tensor_tensor(comb[:, :, :], sc[:, :, :], more[:, :, :], ALU.mult).then_inc(comb_done, 1)

        def tokens_low(b):
            dve.wait_ge(x2_ready, b + 1)
            nc.vector.tensor_tensor(x2_lo[:, b, :], x2T[:, b, :], x2_hi[:, b, :].bitcast(F32), ALU.subtract)\
                .then_inc(x2_low, 1)

        def parts_low(b):
            dve.wait_ge(comb_hi, b + 1)
            nc.vector.tensor_tensor(cparts[b][RW:RW + E_N, :], back_bank(b)[0:E_N, 0:S],
                                    cparts[b][0:E_N, :].bitcast(F32), ALU.subtract).then_inc(parts_done, 1)

        def hidden(g):
            c = CHUNKS[g][1]
            rows = P if c < CH else INTER
            dve.wait_ge(sil_done, g + 1)
            if g >= 3:
                dve.wait_ge(y_done, g - 2)
            h3 = psJ[0:rows, (g % 2) * 512:(g % 2) * 512 + S]
            h = hT[g % 3][0:rows, :]
            if c == CH:
                nc.vector.tensor_tensor(h, sil[g % 2][0:rows, :], h3, ALU.mult).then_inc(h_done, 1)
                return
            nc.vector.tensor_tensor(h, sil[g % 2][0:rows, :], h3, ALU.mult).then_inc(h_part, 1)
            dve.wait_ge(h_part, routed(g) + 1)
            dve.wait_ge(cb_done, routed(g) + 1)
            nc.vector.tensor_tensor(h, h, psT[:, (g % 2) * 512:(g % 2) * 512 + S], ALU.mult).then_inc(h_done, 1)

        def result(b):
            dve.wait_ge(y_done, (b + 1) * NCH)
            nc.vector.tensor_tensor(acc[:, b, :], acc[:, b, :], sum_bank(b), ALU.add).then_inc(res_done, 1)

        rows_out(UNITS - 1, 1)
        token_stats(0)
        token_norm(0)
        norm_out(UNITS - 2)
        gate_groups(0)
        tokens_low(0)
        dve.wait_ge(ld_f, 16 * 4)
        add_out(UNITS - 2, 1)
        gate_experts()
        parts_low(0)
        for g in range(len(CHUNKS)):
            hidden(g)
            if g == 0:
                norm_last(0)
            elif g == 1:
                norm_last(1)
            elif g == 3:
                add_out(UNITS - 1, 1)
                token_stats(1)
            elif g == 4:
                token_norm(1)
            elif g == 6:
                tokens_low(1)
            elif g == 7:
                gate_groups(1)
                gate_experts()
            elif g == 8:
                parts_low(1)
            elif g == NCH + 1:
                result(0)
        result(1)

    @block.tensor
    def _(pe):
        def turn(b):
            for t in range(QT):
                last = nc.tensor.transpose(turn_bank(b)[:, P * t:P * t + P], acc[:, b, P * t:P * t + P], idf[:, :])
            last.then_inc(x2_turned, 1)

        def turn_back(b):
            pe.wait_ge(x2_normed, b + 1)
            for t in range(QT):
                last = nc.tensor.transpose(back_bank(b)[:, P * t:P * t + P], x2n[:, t, :], idf[:, :])
            last.then_inc(x2_back, 1)

        def gate(b):
            pe.wait_ge(ld_f, 16 * 4)
            pe.wait_ge(x2_ready, b + 1)
            for t in range(QT):
                last = nc.tensor.matmul(turn_bank(b)[:, E_N * t:E_N * t + E_N], x2T[:, b, P * t:P * t + P], gw[:, :],
                                        start=True, stop=True)
            last.then_inc(gate_logits, 1)

        def turn_comb(b):
            pe.wait_ge(comb_done, b + 1)
            for t in range(QT):
                last = nc.tensor.transpose(back_bank(b)[0:E_N, P * t:P * t + P], comb[:, t, :], idf[:, :])
            last.then_inc(comb_turned, 1)

        def turn_latents(b, dst):
            for t in range(QT):
                last = nc.tensor.transpose(dst[:, P * t:P * t + P], x_tok[:, QT * b + t, :], idf[:, :])
            last.then_inc(pre_pe, 1)

        def turn_context(b, dst):
            nc.tensor.transpose(dst[:, 0:RW], c_tok[0:RW, b, 1, :], idf[0:RW, 0:RW])
            nc.tensor.transpose(dst[:, RW:RW + P], c_tok[:, b, 0, :], idf[:, :]).then_inc(pre_pe, 1)

        def up(g):
            b, c = CHUNKS[g]
            rows = P if c < CH else INTER
            if g >= 2:
                pe.wait_ge(h_done, g - 1)
            if g % NCH == 0:
                pe.wait_ge(x2_low, b + 1)
                pe.wait_ge(w13_low, 2)
            for k, bank in enumerate((psM, psJ)):
                dst, cols = bank[0:rows, (g % 2) * 512:(g % 2) * 512 + S], slice(P * c, P * c + rows)
                nc.tensor.matmul(dst, w13_hi[:, k, cols], x2_hi[:, b, :], start=True, stop=False)
                nc.tensor.matmul(dst, w13_hi[:, k, cols], x2_lo[:, b, :], start=False, stop=False)
                last = nc.tensor.matmul(dst, w13_lo[:, k, cols], x2_hi[:, b, :], start=False, stop=True)
            last.then_inc(up_done, 1)

        def spread(g):
            b, c = CHUNKS[g]
            if c < CH:
                nc.tensor.matmul(psT[:, (g % 2) * 512:(g % 2) * 512 + S], sel_r[:, P * c:P * c + P], cparts[b][:, :],
                                 start=True, stop=True).then_inc(cb_done, 1)

        def down(g):
            b, c = CHUNKS[g]
            rows = P if c < CH else INTER
            first, last = g % NCH == 0, g % NCH == NCH - 1
            pe.wait_ge(h_done, g + 1)
            nc.tensor.matmul(sum_bank(b), w2s[0:rows, c, :], hT[g % 3][0:rows, :], start=first, stop=last)\
                .then_inc(y_done, 1)

        def parts_product(dst, k, x_hi, x_lo):
            nc.tensor.matmul(dst, wq_hi[:, k, :], x_hi, start=True, stop=False)
            nc.tensor.matmul(dst, wq_hi[:, k, :], x_lo, start=False, stop=False)
            return nc.tensor.matmul(dst, wq_lo[:, k, :], x_hi, start=False, stop=True)

        K_CUT = [((0, 512 - K_AT), (K_AT, 512)), ((512 - K_AT, KC), (512, K_AT + KC))]

        def project_k(b):
            for (lo, hi), (at, end) in K_CUT:
                last = parts_product(psJ[:, at:end], 1, kv_hi[:, b, lo:hi], kv_lo[:, b, lo:hi])
            last.then_inc(k_done, 1)

        def project_q(b):
            lat_cols = slice(C_LAT, C_LAT + S)
            parts_product(psM[:, 0:S], 0, kv_hi[:, b, lat_cols], kv_lo[:, b, lat_cols]).then_inc(q_done, 1)

        def project_v(u, b, bank):
            for t in range(KT):
                nc.tensor.matmul(bank[:, P * t:P * t + P], kvT[:, b, C_MAIN + P * t:C_MAIN + P * t + P], wq[:, 2, :],
                                 start=True, stop=True)
            nc.tensor.matmul(bank[0:2 * RW, MAIN:MAIN + P], kvT[:, b, C_REM2:C_REM2 + 2 * RW], wq[:, 2, :],
                             start=True, stop=True).then_inc(v_done, 1)

        def max_scores(u, par, n, first=False):
            h, t = divmod(n, QT)
            if n == 0:
                pe.wait_ge(q_lo, u + 1)
                pe.wait_ge(k_copied, 2 * u + 2)
            elif n == 1:
                if first:
                    pe.wait_ge(k_lo, 1)
                else:
                    pe.wait_ge(v_out, u + 1)
            else:
                pe.wait_ge(max_done, u * 2 * QT + n - 1)
            for a in range(2):
                lo = RW * h + HALF * a
                last = nc.tensor.matmul((psM, psJ)[n % 2][:, 512 * a:512 * a + HALF], QA[par][:, h, P * t:P * t + P],
                                        KA[par][:, h, lo:lo + HALF], start=True, stop=True)
            last.then_inc(sm_done, 1)

        def max_rows(u):
            pe.wait_ge(m_split, u + 1)
            for t in range(QT):
                last = nc.tensor.matmul(psX[DH:DH + 4, P * t:P * t + P], nmp[:, t, :, :].rearrange("p h a -> p (h a)"),
                                        idb[:, :], start=True, stop=True)
            last.then_inc(mrow_done, 1)

        def score_tile(u, par, n):
            bank = (par * STU + n) % 2
            dst = psT[:, bank * 512:bank * 512 + S]
            if n == 0:
                pe.wait_ge(rows_first, u + 1)
                pe.wait_ge(rows_second, u + 1)
                parts = [(0, MAIN), (1, 0)]
            else:
                if n >= 2:
                    pe.wait_ge(exp_done, u * STU + n - 1)
                h = (n - 1) % 2
                parts = [(h, RW * 2 * h + (n - 1) // 2 * P)]
            for j, (h, lo) in enumerate(parts):
                nc.tensor.matmul(dst, KA[par][:, h, lo:lo + P], QA[par][:, h, :], start=j == 0, stop=False)
                last = nc.tensor.matmul(dst, KB[par][:, h, lo:lo + P], QB[par][:, h, :], start=False, stop=j == len(parts) - 1)
            last.then_inc(st_done, 1)

        def weigh_values(u, par, j, prev=True):
            if j == 0:
                if prev:
                    pe.wait_ge(o_out, u)
                pe.wait_ge(v_out, u + 1)
            for h in range(2):
                cols = slice(DH * h, DH * h + DH)
                pe.wait_ge(exp_done, u * STU + (1 if j == 0 else 2 * j + h))
                if j == 0:
                    v, p = VR[par][:, cols], PRr[par][:, :]
                else:
                    v, p = V[par][:, j - 1, cols], PR[par][:, j - 1, h, :]
                last = nc.tensor.matmul(psO[cols, :], v, p, start=j == 0, stop=j == KT)
            if j == KT:
                last.then_inc(pv_done, 1)

        def denominators(u, par):
            pe.wait_ge(sum_done, u + 1)
            for h in range(2):
                last = nc.tensor.matmul(psX[DH * h:DH * h + DH, :], ones[:, :], SUM[par][:, h, :], start=True, stop=True)
            last.then_inc(den_done, 1)

        def project_out(u):
            pe.wait_ge(on_done, u + 1)
            nc.tensor.matmul(psX[:, :], wop[:, :], on[:, :], start=True, stop=True).then_inc(wo_done, 1)

        def unit(u, par, nb, prev=True, first=False):
            other = 1 - par
            pe.wait_ge(wq_low, u + 1)
            pe.wait_ge(max_done, u * 2 * QT + 2 * QT - 1)
            project_q(nb)
            if not first:
                pe.wait_ge(acc_done, u - 1)
            max_rows(u)
            if prev:
                weigh_values(u - 1, other, KT)
            project_k(nb)
            score_tile(u, par, 0)
            score_tile(u, par, 1)
            if prev:
                denominators(u - 1, other)
            else:
                pe.wait_ge(pool_normed, 2 * QT)
                turn_latents(1, psX)
            score_tile(u, par, 2)
            score_tile(u, par, 3)
            weigh_values(u, par, 0, prev)
            score_tile(u, par, 4)
            pe.wait_ge(k_lo, u + 2)
            project_v(u + 1, nb, psJ)
            max_scores(u + 1, other, 0)
            score_tile(u, par, 5)
            weigh_values(u, par, 1)
            max_scores(u + 1, other, 1)
            score_tile(u, par, 6)
            weigh_values(u, par, 2)
            max_scores(u + 1, other, 2)
            score_tile(u, par, 7)
            max_scores(u + 1, other, 3)
            if prev:
                pe.wait_ge(ld_wo, 16 * u)
                project_out(u - 1)
            else:
                pe.wait_ge(kv_ready, 3)
                pe.wait_ge(con_normed, 1)
                turn_context(1, psX)
            max_scores(u + 1, other, 4)
            weigh_values(u, par, 3)
            score_tile(u, par, 8)
            max_scores(u + 1, other, 5)
            score_tile(u, par, 9)
            max_scores(u + 1, other, 6)
            score_tile(u, par, 10)
            max_scores(u + 1, other, 7)
            weigh_values(u, par, 4)

        def last_unit():
            u, par = UNITS - 1, 1
            weigh_values(u - 1, 0, KT)
            pe.wait_ge(max_done, u * 2 * QT + 2 * QT - 1)
            turn(0)
            pe.wait_ge(acc_done, u - 1)
            max_rows(u)
            score_tile(u, par, 0)
            denominators(u - 1, 0)
            score_tile(u, par, 1)
            turn_back(0)
            score_tile(u, par, 2)
            score_tile(u, par, 3)
            weigh_values(u, par, 0)
            score_tile(u, par, 4)
            score_tile(u, par, 5)
            gate(0)
            weigh_values(u, par, 1)
            weigh_values(u, par, 2)
            score_tile(u, par, 6)
            score_tile(u, par, 7)
            pe.wait_ge(ld_wo, 16 * u)
            project_out(u - 1)
            score_tile(u, par, 8)
            weigh_values(u, par, 3)
            score_tile(u, par, 9)
            pe.wait_ge(scores_done, 1)
            up(0)
            score_tile(u, par, 10)
            weigh_values(u, par, 4)
            weigh_values(u, par, 5)
            turn_comb(0)

        pe.wait_ge(ld_s, 16 * 2)
        pe.wait_ge(rows_normed, 1)
        turn_context(0, psT)
        pe.wait_ge(rows_normed, 2)
        turn_latents(0, psM)

        pe.wait_ge(kv_ready, 1)
        pe.wait_ge(ld_qkv, 16)
        nc.tensor.matmul(psM[:, 0:S], wq[:, 0, :], kvT[:, 0, C_LAT:C_LAT + S], start=True, stop=True).then_inc(q_done, 1)
        pe.wait_ge(kv_ready, 2)
        for (lo, hi), (at, end) in K_CUT:
            last = nc.tensor.matmul(psJ[:, at:end], wq[:, 1, :], kvT[:, 0, lo:hi], start=True, stop=True)
        last.then_inc(k_done, 1)
        project_v(0, 0, psT)
        pe.wait_ge(consts_ready, 1)
        for n in range(2 * QT):
            max_scores(0, 0, n, first=True)
        pe.wait_ge(kv_low, 1)
        unit(0, 0, 0, prev=False, first=True)
        unit(1, 1, 0, first=True)
        unit(2, 0, 0)
        with pe.Fori(1, PAIRS // 2 - 1) as i:
            unit(2 * i + 1, 1, 0)
            unit(2 * i + 2, 0, 0)
        pe.wait_ge(kv_ready, 4)
        pe.wait_ge(kv_low, 2)
        unit(PAIRS - 1, 1, 1)
        unit(PAIRS, 0, 1)
        with pe.Fori(PAIRS // 2, PAIRS - 1) as i:
            unit(2 * i + 1, 1, 1)
            unit(2 * i + 2, 0, 1)
        last_unit()

        pe.wait_ge(parts_done, 1)
        up(1)
        pe.wait_ge(sel_ready, 1)
        spread(0)
        pe.wait_ge(o_out, UNITS)
        denominators(UNITS - 1, 1)
        spread(1)
        for g in range(2, len(CHUNKS)):
            up(g)
            if g == NCH + 1:
                pe.wait_ge(parts_done, 2)
            spread(g)
            if g == 3:
                pe.wait_ge(ld_wo, 16 * UNITS)
                project_out(UNITS - 1)
            elif g == 4:
                pe.wait_ge(acc_done, UNITS)
                turn(1)
            elif g == 6:
                turn_back(1)
            elif g == 7:
                gate(1)
            elif g == 9:
                turn_comb(1)
            down(g - 2)
        down(len(CHUNKS) - 2)
        down(len(CHUNKS) - 1)


def kernel(x, ctx_1024, mask_BxS2_bf1, L0_xattn_gm, L0_xattn_bm, L0_xattn_gl, L0_xattn_bl, L0_xattn_Wq, L0_xattn_Wk,
           L0_xattn_Wv, L0_xattn_Wo, L0_ffn_gate_w, L0_ffn_gate_bias, L0_ffn_w1, L0_ffn_w2, L0_ffn_w3, L0_ffn_ws1,
           L0_ffn_ws2, L0_ffn_ws3):
    import concourse.bacc as bacc
    import numpy as np
    from concourse.bass_utils import run_bass_kernel_spmd

    a = np.asarray
    xt = a(x).reshape(B * S, D)

    def by_pair(w):
        return a(w).reshape(D, PAIRS, P)

    own = np.zeros((4, 2, KEYS), np.float32)
    own[0:2, 0], own[2:4, 1] = 1.0, 1.0
    sel = np.zeros((RW + E_N, CH * P), np.float32)
    for part in range(2):
        for e in range(E_N):
            sel[RW * part + e, e * INTER:(e + 1) * INTER] = 1.0
    arrays = {
        "xt": xt,
        "xT": xt.T,
        "cx": a(ctx_1024),
        "mask": a(mask_BxS2_bf1).view(np.uint8),
        "maskT": a(mask_BxS2_bf1).view(np.uint8).T,
        "lngb": np.stack([a(L0_xattn_gm), a(L0_xattn_bm), a(L0_xattn_gl), a(L0_xattn_bl)], axis=1),
        "wqkv": np.stack([by_pair(L0_xattn_Wq), by_pair(L0_xattn_Wk), by_pair(L0_xattn_Wv)], axis=2).transpose(1, 0, 2, 3),
        "wo": a(L0_xattn_Wo).reshape(PAIRS, P, D),
        "gate_w": a(L0_ffn_gate_w).T,
        "gate_b": a(L0_ffn_gate_bias),
        "w1": np.concatenate([a(L0_ffn_w1).transpose(2, 0, 1).reshape(D, E_N * INTER), a(L0_ffn_ws1).T], axis=1),
        "w3": np.concatenate([a(L0_ffn_w3).transpose(2, 0, 1).reshape(D, E_N * INTER), a(L0_ffn_ws3).T], axis=1),
        "w2": a(L0_ffn_w2).transpose(0, 2, 1).reshape(E_N * INTER, D),
        "ws2": a(L0_ffn_ws2).T,
        "ident": np.eye(P, dtype=np.float32),
        "sel": sel,
        "own": own,
    }
    arrays = {"in_" + k: np.ascontiguousarray(v) for k, v in arrays.items()}
    nc = bacc.Bacc("TRN2", target_bir_lowering=False, num_devices=1)
    aps = [nc.dram_tensor(k, v.shape, mybir.dt.from_np(v.dtype), kind="ExternalInput").ap() for k, v in arrays.items()]
    out = nc.dram_tensor("out_T", (D, B * S), F32, kind="ExternalOutput").ap()
    with ExitStack() as ctx:
        build(nc, ctx, *aps, out)
    got = run_bass_kernel_spmd(nc, [arrays], core_ids=[0]).results[0]["out_T"]
    return np.ascontiguousarray(got.T).reshape(B, S, D)
```
